# Optimizing a Trainium2 kernel written in Bass

```python
import numpy as np
import jax
import jax.numpy as jnp

def _softmax(x, axis=-1):
    return jax.nn.softmax(x, axis=axis)

def _gelu(x):
    return jax.nn.gelu(x, approximate=True)

def _silu(x):
    return jax.nn.silu(x)

def _sigmoid(x):
    return jax.nn.sigmoid(x)

def _layernorm(x, axis=-1, eps=1e-05):
    m = jnp.mean(x, axis=axis, keepdims=True)
    v = jnp.var(x, axis=axis, keepdims=True)
    return (x - m) / jnp.sqrt(v + eps)

def _scatter_add(tgt, idx, src, axis=0):
    return tgt.at[idx].add(src)

def _segment_sum(src, seg, n):
    return jax.ops.segment_sum(src, seg, n)
kernel_name = 'mk_adj_resnorm_d4_adj_r2_63b20f'

def setup_inputs(seed: int=0):
    np.random.seed(seed)
    _w = jnp.asarray

    def _rec_inputs():
        import jax
        import jax.numpy as jnp
        _gk = jax.random.key(seed)
        x = -0.0005207 + 1.001 * jax.random.normal(jax.random.fold_in(_gk, 1), (64, 128, 128), jnp.float32)
        _a = jax.random.bernoulli(jax.random.fold_in(_gk, 2), 0.125, (64, 128, 128))
        _a = jnp.logical_or(_a, jnp.swapaxes(_a, -1, -2))
        _a = jnp.logical_or(_a, jnp.eye(128, dtype=bool))
        _af = _a.astype(jnp.float32)
        _af = _af * jax.random.uniform(jax.random.fold_in(_gk, 3), (64, 128, 128), jnp.float32, 0.05, 1)
        adj = _af
        return (x, adj)
    x, adj = _rec_inputs()

    def _L0_gnn_setup():
        import jax, jax.numpy as jnp
        import numpy as np
        key = jax.random.key(seed)
        k1, k2, k3, k4 = jax.random.split(key, 4)
        B, N, D = (8, 1024, 128)
        embeddings = jax.random.normal(k1, (B, N, D), dtype=jnp.float32)
        adjacency_matrix = jax.random.uniform(k2, (B, N, N), dtype=jnp.float32)
        cost_matrix = jax.random.uniform(k3, (B, N, N), dtype=jnp.float32)
        W = jax.random.normal(k4, (D, 2 * D), dtype=jnp.float32) * (1.0 / np.sqrt(2 * D))
        b = jnp.zeros((D,), dtype=jnp.float32)
        return {'embeddings': embeddings, 'adjacency_matrix': adjacency_matrix, 'cost_matrix': cost_matrix, 'W': W, 'b': b}
    _L0_gnn_all = _L0_gnn_setup()
    _L0_gnn_in = {k: v for k, v in _L0_gnn_all.items() if k in ('W', 'b')}
    del _L0_gnn_all

    def _L1_gnn_setup():
        import jax, jax.numpy as jnp
        import numpy as np
        NEG_SLOPE = 0.2
        key = jax.random.key(seed)
        k1, k2, k3, k4 = jax.random.split(key, 4)
        B, n, d_in, d_out = (8, 1024, 128, 128)
        x = jax.random.normal(k1, (B, n, d_in), dtype=jnp.float32)
        adj = jax.random.uniform(k2, (B, n, n), dtype=jnp.float32)
        W = jax.random.normal(k3, (d_in, d_out), dtype=jnp.float32) * np.sqrt(2.0 / (d_in + d_out))
        a = jax.random.normal(k4, (2 * d_out,), dtype=jnp.float32) * np.sqrt(2.0 / (2 * d_out + 1))
        return {'x': x, 'adj': adj, 'W': W, 'a': a}
    _L1_gnn_all = _L1_gnn_setup()
    _L1_gnn_in = {k: v for k, v in _L1_gnn_all.items() if k in ('W', 'a')}
    del _L1_gnn_all

    def _L2_gnn_setup():
        import jax, jax.numpy as jnp
        import numpy as np
        key = jax.random.key(seed)
        k1, k2, k3 = jax.random.split(key, 3)
        B, N, Din, Dout = (8, 2048, 128, 128)
        x = jax.random.normal(k1, (B, N, Din), dtype=jnp.float32)
        adj = jax.random.uniform(k2, (B, N, N), dtype=jnp.float32)
        limit = float(np.sqrt(6.0 / (Din + Dout)))
        weight = jax.random.uniform(k3, (Din, Dout), dtype=jnp.float32, minval=-limit, maxval=limit)
        bias = jnp.zeros((Dout,), dtype=jnp.float32)
        return {'x': x, 'adj': adj, 'weight': weight, 'bias': bias}
    _L2_gnn_all = _L2_gnn_setup()
    _L2_gnn_in = {k: v for k, v in _L2_gnn_all.items() if k in ('weight', 'bias')}
    del _L2_gnn_all

    def _L3_gnn_setup():
        import jax, jax.numpy as jnp
        import numpy as np
        B, S, H, HID = (1, 512, 128, 128)
        LN_EPS = 1e-05

        def _layernorm(y, gamma, beta):
            mu = jnp.mean(y, axis=-1, keepdims=True)
            var = jnp.mean(jnp.square(y - mu), axis=-1, keepdims=True)
            return (y - mu) * jax.lax.rsqrt(var + LN_EPS) * gamma + beta
        key = jax.random.key(seed)
        ks = jax.random.split(key, 8)
        x = jax.random.normal(ks[0], (B, S, H), dtype=jnp.float32)
        adj = jax.random.uniform(ks[1], (B, S, S), dtype=jnp.float32)
        W1 = jax.random.normal(ks[2], (2 * H, HID), dtype=jnp.float32) / np.sqrt(2 * H)
        b1 = jnp.zeros((HID,), dtype=jnp.float32)
        W2 = jax.random.normal(ks[3], (HID, HID), dtype=jnp.float32) / np.sqrt(HID)
        b2 = jnp.zeros((HID,), dtype=jnp.float32)
        gamma = jnp.ones((HID,), dtype=jnp.float32)
        beta = jnp.zeros((HID,), dtype=jnp.float32)
        return {'x': x, 'adj': adj, 'W1': W1, 'b1': b1, 'W2': W2, 'b2': b2, 'gamma': gamma, 'beta': beta}
    _L3_gnn_all = _L3_gnn_setup()
    _L3_gnn_in = {k: v for k, v in _L3_gnn_all.items() if k in ('W1', 'b1', 'W2', 'b2', 'gamma', 'beta')}
    del _L3_gnn_all
    return {'x': x, 'adj': adj, 'L0_gnn_W': _L0_gnn_in['W'], 'L0_gnn_b': _L0_gnn_in['b'], 'L1_gnn_W': _L1_gnn_in['W'], 'L1_gnn_a': _L1_gnn_in['a'], 'L2_gnn_weight': _L2_gnn_in['weight'], 'L2_gnn_bias': _L2_gnn_in['bias'], 'L3_gnn_W1': _L3_gnn_in['W1'], 'L3_gnn_b1': _L3_gnn_in['b1'], 'L3_gnn_W2': _L3_gnn_in['W2'], 'L3_gnn_b2': _L3_gnn_in['b2'], 'L3_gnn_gamma': _L3_gnn_in['gamma'], 'L3_gnn_beta': _L3_gnn_in['beta']}

def reference(x, adj, L0_gnn_W, L0_gnn_b, L1_gnn_W, L1_gnn_a, L2_gnn_weight, L2_gnn_bias, L3_gnn_W1, L3_gnn_b1, L3_gnn_W2, L3_gnn_b2, L3_gnn_gamma, L3_gnn_beta):
    import jax
    import jax.numpy as jnp

    def _L0_gnn_ref(embeddings, adjacency_matrix, cost_matrix, W, b):
        import jax, jax.numpy as jnp
        import numpy as np
        degree = adjacency_matrix.sum(axis=-1)[:, :, None]
        sum_neighbors = jnp.einsum('bid,bij->bjd', embeddings, cost_matrix) / degree
        concatenated = jnp.concatenate([embeddings, sum_neighbors], axis=-1)
        out = jnp.einsum('bnk,dk->bnd', concatenated, W) + b
        return jax.nn.relu(out)

    def _L1_gnn_ref(x, adj, W, a):
        import jax, jax.numpy as jnp
        import numpy as np
        NEG_SLOPE = 0.2
        d_out = W.shape[1]
        h = jnp.einsum('bni,io->bno', x, W)
        x_weighted = jnp.einsum('bnm,bmo->bno', adj, h)
        a_src, a_dst = (a[:d_out], a[d_out:])
        s_i = h @ a_src
        s_j = h @ a_dst
        e = jax.nn.leaky_relu(s_i[:, :, None] + s_j[:, None, :], NEG_SLOPE)
        alpha = jax.nn.softmax(e, axis=2)
        out = jnp.einsum('bnm,bmo->bno', alpha, h) + x_weighted
        return jax.nn.leaky_relu(out, NEG_SLOPE)

    def _L2_gnn_ref(x, adj, weight, bias):
        import jax, jax.numpy as jnp
        import numpy as np
        B, N, _ = x.shape
        adj = adj + jnp.eye(N, dtype=adj.dtype)[None]
        degree = adj.sum(axis=2)
        d_inv_sqrt = degree ** (-0.5)
        d_inv_sqrt = jnp.where(jnp.isinf(d_inv_sqrt), 0.0, d_inv_sqrt)
        adj_norm = d_inv_sqrt[:, :, None] * adj * d_inv_sqrt[:, None, :]
        support = jnp.einsum('bnd,de->bne', x, weight)
        out = jnp.einsum('bnm,bme->bne', adj_norm, support) + bias
        return out

    def _L3_gnn_ref(x, adj, W1, b1, W2, b2, gamma, beta):
        import jax, jax.numpy as jnp
        import numpy as np
        B, S, H, HID = (1, 512, 128, 128)
        LN_EPS = 1e-05

        def _layernorm(y, gamma, beta):
            mu = jnp.mean(y, axis=-1, keepdims=True)
            var = jnp.mean(jnp.square(y - mu), axis=-1, keepdims=True)
            return (y - mu) * jax.lax.rsqrt(var + LN_EPS) * gamma + beta
        hi = jnp.einsum('bsh,hk->bsk', x, W1[:H])
        hj = jnp.einsum('bsh,hk->bsk', x, W1[H:])
        h = jax.nn.relu(hi[:, :, None, :] + hj[:, None, :, :] + b1)
        y = jnp.einsum('bijk,kl->bijl', h, W2) + b2
        y = _layernorm(y, gamma, beta)
        out = jnp.einsum('bij,bijh->bih', adj, y)
        return out
    x = _layernorm(x + _L0_gnn_ref(x, adj, adj, L0_gnn_W, L0_gnn_b), axis=-1)
    x = _layernorm(x + _L1_gnn_ref(x, adj, L1_gnn_W, L1_gnn_a), axis=-1)
    x = _layernorm(x + _L2_gnn_ref(x, adj, L2_gnn_weight, L2_gnn_bias), axis=-1)
    x = _layernorm(x + _L3_gnn_ref(x, adj, L3_gnn_W1, L3_gnn_b1, L3_gnn_W2, L3_gnn_b2, L3_gnn_gamma, L3_gnn_beta), axis=-1)
    return x

_drawn_inputs = setup_inputs


def setup_inputs(seed=0):
    import zlib

    import numpy as np

    out = dict(_drawn_inputs(seed))
    spreads = {'L0_gnn_b': (0.0, 0.1),
     'L2_gnn_bias': (0.0, 0.1),
     'L3_gnn_b1': (0.0, 0.1),
     'L3_gnn_b2': (0.0, 0.1),
     'L3_gnn_gamma': (1.0, 0.2),
     'L3_gnn_beta': (0.0, 0.1)}
    factors = {}
    for name, (base, spread) in spreads.items():
        noise = np.random.default_rng([zlib.crc32(name.encode()), seed]).standard_normal(out[name].shape)
        drawn = base * np.exp(spread * noise) if base else spread * noise
        out[name] = jnp.asarray(drawn.astype(out[name].dtype))
    for name, factor in factors.items():
        out[name] = (out[name] * factor).astype(out[name].dtype)
    return out
```

```python
from contextlib import ExitStack

import concourse.bass as bass
from concourse import mybir

F32 = mybir.dt.float32
BF16 = mybir.dt.bfloat16
ALU = mybir.AluOpType
ACT = mybir.ActivationFunctionType
AX = mybir.AxisListType

EPS = 1e-5
SLOPE = 0.2


def graph_layers_kernel(nc, x, adj, w0, b0, w1, a1, w2, b2, e_w1, e_b1, e_w2, e_b2, e_gamma, e_beta, out):
    GRAPHS, N, D = x.shape
    P = 128
    assert N == P and D == P
    G = 4
    GROUPS = GRAPHS // G
    GW = G * P
    J = 8
    CHUNKS = P // J
    BANK = 4
    WIDE = 3
    HR = 4
    AHEAD = 2
    ZSLOT = [c % 3 for c in range(CHUNKS - 1)] + [1]

    def previous(slots, c):
        for back in range(1, CHUNKS + 1):
            if slots[(c - back) % CHUNKS] == slots[c]:
                return (0 if c - back >= 0 else 1), (c - back) % CHUNKS

    with ExitStack() as ctx:
        def sb(name, shape, dt=F32):
            return ctx.enter_context(nc.sbuf_tensor(name, shape, dt))

        def sem(name):
            return ctx.enter_context(nc.semaphore(name))

        adj_all = sb("adj_all", [P, GRAPHS, P])
        x_all = sb("x_all", [P, GRAPHS, P])
        aT_all = sb("aT_all", [P, GRAPHS, P])
        bT_all = sb("bT_all", [P, GRAPHS, P])
        ident = sb("ident", [P, P])
        ones16 = sb("ones16", [P, P], BF16)
        w0_sb = sb("w0_sb", [P, 2 * P])
        w0T = sb("w0T", [P, 2, P])
        w1_sb = sb("w1_sb", [P, P])
        a1B = sb("a1B", [P, 2 * P])
        u = sb("u", [P, 2])
        u_dstB = sb("u_dstB", [P, P])
        w2_sb = sb("w2_sb", [P, P])
        b2B = sb("b2B", [P, P])
        e_w1_sb = sb("e_w1_sb", [P, 2, P])
        e_b1_sb = sb("e_b1_sb", [P, 1])
        e_w2_sb = sb("e_w2_sb", [P, P])
        w2c = sb("w2c", [P, P])
        rowB = sb("rowB", [P, 2, P])
        rowT = sb("rowT", [P, 2, P])
        rowH = sb("rowH", [P, 3, 2, P], BF16)
        bias16 = sb("bias16", [P, 2, BANK, P], BF16)
        gammaB = sb("gammaB", [P, P])
        betaB = sb("betaB", [P, P])
        mean_c = sb("mean_c", [P, 2])
        eps_c = sb("eps_c", [P, 1])
        half_c = sb("half_c", [P, G])
        xq = sb("xq", [P, G, P])
        adjq = sb("adjq", [P, G, P])
        xT = sb("xT", [P, G, P])
        proj = sb("proj", [P, G, P])
        y0 = sb("y0", [P, G, P])
        x1T = sb("x1T", [P, G, P])
        h1 = sb("h1", [P, G, P])
        att = sb("att", [P, G, P])
        attT = sb("attT", [P, G, P])
        y1 = sb("y1", [P, G, P])
        x2T = sb("x2T", [P, G, P])
        adjr = sb("adjr", [P, G, P])
        adjT = sb("adjT", [P, G, P])
        supp = sb("supp", [P, G, P])
        y2 = sb("y2", [P, G, P])
        x2b = sb("x2b", [P, G, P])
        x3T = sb("x3T", [P, G, P])
        deg = sb("deg", [P, GRAPHS])
        rdeg = sb("rdeg", [P, G])
        dis = sb("dis", [P, GRAPHS])
        dtmp = sb("dtmp", [P, 3, G])
        src = sb("src", [P, G])
        soft = sb("soft", [P, 5, G])
        lnst = [sb(f"lnst{k}", [P, G, 6]) for k in range(3)]
        lnmv = [sb(f"lnmv{k}", [P, G, 2]) for k in range(3)]
        lnve = [sb(f"lnve{k}", [P, G]) for k in range(3)]
        lnrs = [sb(f"lnrs{k}", [P, G]) for k in range(3)]
        hid = sb("hid", [P, HR, J, P])
        sq = sb("sq", [P, 2, WIDE, P])
        junk = sb("junk", [P, J - WIDE, P])
        ss = sb("ss", [P, 2, J])
        sd = sb("sd", [P, 2, J])
        rs = sb("rs", [P, 2, J])
        wt = sb("wt", [P, 2, J])
        acc = sb("acc", [P, 2, P])
        fin = sb("fin", [P, 3, P])
        carrier = sb("carrier", [P, 2])
        fst = sb("fst", [P, 6])
        fmv = sb("fmv", [P, 2])
        fsd = sb("fsd", [P, 2])
        res = sb("res", [P, P])

        bank = [ctx.enter_context(nc.psum_tensor(f"bank{k}", [P, 512], F32)) for k in range(8)]

        def graphs_of(k):
            return bank[k][:, :].rearrange("p (g n) -> p g n", g=G)

        def per_graph(t):
            return t[:, :].unsqueeze(2).to_broadcast([P, G, P])

        s_w = sem("weights_loaded")
        s_cst = sem("constants_set")
        s_wT = sem("w0_transposed")
        s_set = sem("setup_step")
        s_wready = sem("weights_ready")
        s_xq = sem("x_group_loaded")
        s_aq = sem("adj_group_loaded")
        s_r = sem("adj_again_loaded")
        s_all = sem("kept_inputs_loaded")
        s_xt = sem("xT_in_psum")
        s_xte = sem("xT_ready")
        s_xp = sem("self_and_neighbour_products")
        s_pe = sem("proj_ready")
        s_ag = sem("aggregated_in_psum")
        s_d0 = sem("vector_L0_step")
        s_rs = [sem(f"rsqrt_ready{k}") for k in range(3)]
        s_ve = [sem(f"variance_ready{k}") for k in range(3)]
        s_ds = sem("degree_shifted")
        s_dp = sem("degree_power")
        s_dis = sem("dis_ready")
        s_x1 = sem("x1_ready")
        s_x1k = sem("x1_kept")
        s_x1t = sem("x1T_in_psum")
        s_x1e = sem("x1T_ready")
        s_h = sem("h_and_scores_in_psum")
        s_he = sem("h_ready")
        s_src = sem("src_score_ready")
        s_d1 = sem("vector_L1_step")
        s_nm = sem("scores_ready")
        s_ex = sem("exp_ready")
        s_att = sem("attention_ready")
        s_at = sem("attention_T_in_psum")
        s_ate = sem("attention_T_ready")
        s_mh = sem("attended_in_psum")
        s_rl = sem("attended_relu_ready")
        s_xr = sem("x1_plus_relu_ready")
        s_x2 = sem("x2_ready")
        s_x2k = sem("x2_kept")
        s_x2t = sem("x2T_in_psum")
        s_x2e = sem("x2T_ready")
        s_tr = sem("adjT_in_psum")
        s_tre = sem("adjT_ready")
        s_su = sem("support_in_psum")
        s_sue = sem("support_ready")
        s_xb = sem("x2_plus_bias_ready")
        s_cv = sem("convolved_in_psum")
        s_d2 = sem("vector_L2_step")
        s_x3 = sem("x3_ready")
        s_x3t = sem("x3T_in_psum")
        s_x3e = sem("x3T_ready")
        s_ab = sem("a_and_b_in_psum")
        s_abe = sem("a_and_b_ready")
        s_x3b = sem("residual_ready")
        s_bt = sem("beta_times_degree")
        s_pre = sem("sums_ready")
        s_hid = sem("hidden_ready")
        s_z = sem("z_bank_ready")
        s_sq = sem("squares_ready")
        s_red = sem("squares_summed")
        s_ac = sem("accumulated_squares")
        s_sd = sem("deviation_ready")
        s_wk = sem("weight_step")
        s_acc = sem("z_accumulated")
        s_fin = sem("finish_step")
        s_fsd = sem("finish_deviation")
        s_res = sem("result_ready")
        s_out = sem("result_stored")

        def cols(t, q):
            return t[:, bass.ds(q * G, G), :]

        block = ctx.enter_context(nc.Block())

        @block.sync
        def _(sp):
            def row(ap):
                return ap.rearrange("(a n) -> a n", a=1).to_broadcast([P, ap.shape[0]])

            for dst, s in ((w0_sb[:, :], w0), (w1_sb[:, :], w1), (w2_sb[:, :], w2),
                           (e_w1_sb[:, :, :], e_w1.rearrange("(t h) k -> h t k", t=2)),
                           (e_w2_sb[:, :], e_w2), (e_b1_sb[:, :], e_b1.rearrange("(k a) -> k a", a=1)),
                           (a1B[:, :], row(a1)), (b2B[:, :], row(b2)), (gammaB[:, :], row(e_gamma)),
                           (betaB[:, :], row(e_beta)), (rowB[:, 0, :], row(b0)), (rowB[:, 1, :], row(e_b2))):
                sp.dma_start(dst, s).then_inc(s_w, 16)

            def group(t, q):
                return t[bass.ds(q * G, G), :, :].rearrange("g n d -> n g d")

            def kept(q):
                sp.wait_ge(s_all, q * 32)
                sp.dma_start(cols(x_all, q), group(x, q)).then_inc(s_all, 16)
                sp.dma_start(cols(adj_all, q), group(adj, q)).then_inc(s_all, 16)

            def for_l0(q):
                sp.wait_ge(s_xq, q * 16)
                sp.wait_ge(s_xt, q)
                sp.dma_start(xq[:, :, :], group(x, q)).then_inc(s_xq, 16)
                sp.wait_ge(s_aq, q * 16)
                sp.wait_ge(s_ag, q)
                sp.dma_start(adjq[:, :, :], group(adj, q)).then_inc(s_aq, 16)

            def for_l2(q):
                sp.wait_ge(s_r, q * 16)
                sp.wait_ge(s_tr, q)
                sp.dma_start(adjr[:, :, :], group(adj, q)).then_inc(s_r, 16)

            for_l0(0)
            kept(0)
            with sp.Fori(1, GROUPS) as q:
                kept(q)
                for_l0(q)
                for_l2(q - 1)
            for_l2(GROUPS - 1)
            with sp.Fori(0, GRAPHS) as b:
                sp.wait_ge(s_res, b + 1)
                sp.dma_start(out[bass.ds(b, 1), :, :].rearrange("g n d -> n (g d)"), res[:, :]).then_inc(s_out, 16)
            sp.wait_ge(s_out, 16 * GRAPHS)

        @block.tensor
        def _(pe):
            def transposes(k, source):
                for g in range(G):
                    last = nc.tensor.transpose(bank[k][:, g * P:(g + 1) * P], source[:, g, :], ident[:, :])
                return last

            pe.wait_ge(s_w, 16 * 12)
            pe.wait_ge(s_cst, 1)
            nc.tensor.transpose(bank[0][:, 0:P], w0_sb[:, 0:P], ident[:, :])
            nc.tensor.transpose(bank[0][:, P:2 * P], w0_sb[:, P:2 * P], ident[:, :]).then_inc(s_wT, 1)
            pe.wait_ge(s_wready, 1)

            def l0_transpose(q):
                pe.wait_ge(s_xq, (q + 1) * 16)
                pe.wait_ge(s_x1e, q)
                transposes(0, xq).then_inc(s_xt, 1)

            def l0_project(q):
                pe.wait_ge(s_xte, q + 1)
                pe.wait_ge(s_ve[0], q)
                nc.tensor.matmul(bank[1][:, :], ones16[:, :], bias16[:, 0, :, :], start=True, stop=False,
                                 skip_group_check=True)
                for g in range(G):
                    nc.tensor.matmul(bank[1][:, g * P:(g + 1) * P], xT[:, g, :], w0T[:, 0, :],
                                     start=False, stop=(g == G - 1), skip_group_check=True)
                for g in range(G):
                    last = nc.tensor.matmul(bank[2][:, g * P:(g + 1) * P], xT[:, g, :], w0T[:, 1, :],
                                            start=True, stop=True)
                last.then_inc(s_xp, 1)

            def l0_aggregate(q):
                pe.wait_ge(s_aq, (q + 1) * 16)
                pe.wait_ge(s_pe, q + 1)
                for g in range(G):
                    last = nc.tensor.matmul(bank[2][:, g * P:(g + 1) * P], adjq[:, g, :], proj[:, g, :],
                                            start=True, stop=True)
                last.then_inc(s_ag, 1)

            def l0_x1T(q):
                pe.wait_ge(s_x1, q + 1)
                transposes(0, y0).then_inc(s_x1t, 1)

            def l1_scores(q):
                pe.wait_ge(s_x1e, q + 1)
                pe.wait_ge(s_d1, q)
                for g in range(G):
                    nc.tensor.matmul(bank[3][:, g * P:(g + 1) * P], x1T[:, g, :], w1_sb[:, :], start=True, stop=True)
                pe.wait_ge(s_ate, q)
                nc.tensor.matmul(bank[4][:, :], u_dstB[:, :], x1T[:, :, :], start=True, stop=True)
                pe.wait_ge(s_x2e, q)
                for g in range(G):
                    last = nc.tensor.matmul(bank[5][:, 2 * g:2 * g + 2], x1T[:, g, :], u[:, 0:2],
                                            start=True, stop=True)
                last.then_inc(s_h, 1)

            def l1_transpose(q):
                pe.wait_ge(s_att, q + 1)
                transposes(4, att).then_inc(s_at, 1)

            def l1_attend(q):
                pe.wait_ge(s_ate, q + 1)
                pe.wait_ge(s_he, q + 1)
                for g in range(G):
                    last = nc.tensor.matmul(bank[3][:, g * P:(g + 1) * P], attT[:, g, :], h1[:, g, :],
                                            start=True, stop=True)
                last.then_inc(s_mh, 1)

            def l1_x2T(q):
                pe.wait_ge(s_x2, q + 1)
                transposes(5, y1).then_inc(s_x2t, 1)

            def l2_adjT(q):
                pe.wait_ge(s_r, (q + 1) * 16)
                pe.wait_ge(s_abe, q)
                transposes(6, adjr).then_inc(s_tr, 1)

            def l2_support(q):
                pe.wait_ge(s_x2e, q + 1)
                for g in range(G):
                    last = nc.tensor.matmul(bank[7][:, g * P:(g + 1) * P], x2T[:, g, :], w2_sb[:, :],
                                            start=True, stop=True)
                last.then_inc(s_su, 1)

            def l2_convolve(q):
                pe.wait_ge(s_tre, q + 1)
                pe.wait_ge(s_sue, q + 1)
                for g in range(G):
                    last = nc.tensor.matmul(bank[6][:, g * P:(g + 1) * P], adjT[:, g, :], supp[:, g, :],
                                            start=True, stop=True)
                last.then_inc(s_cv, 1)

            def l2_x3T(q):
                pe.wait_ge(s_x3, q + 1)
                transposes(7, y2).then_inc(s_x3t, 1)

            def l3_inputs(q):
                pe.wait_ge(s_x3e, q + 1)
                nc.tensor.matmul(bank[6][:, :], e_w1_sb[:, 0, :], x3T[:, :, :], start=True, stop=True)
                nc.tensor.matmul(bank[7][:, :], e_w1_sb[:, 1, :], x3T[:, :, :], start=True, stop=True)\
                    .then_inc(s_ab, 1)

            def layers(t, l0, l1, l2):
                if l2: l2_adjT(t - 2)
                if l0: l0_transpose(t)
                if l1: l1_scores(t - 1)
                if l2: l2_support(t - 2)
                if l0: l0_project(t)
                if l2: l2_convolve(t - 2)
                if l1: l1_transpose(t - 1)
                if l0: l0_aggregate(t)
                if l1: l1_attend(t - 1)
                if l2: l2_x3T(t - 2)
                if l2: l3_inputs(t - 2)
                if l0: l0_x1T(t)
                if l1: l1_x2T(t - 1)

            layers(0, True, False, False)
            layers(1, True, True, False)
            with pe.Fori(2, GROUPS) as t:
                layers(t, True, True, True)
            layers(GROUPS, False, True, True)
            layers(GROUPS + 1, False, False, True)

            pe.wait_ge(s_abe, GROUPS)
            pe.wait_ge(s_ve[0], GROUPS)
            pe.wait_ge(s_d1, GROUPS)

            def edge_graph(b, first):
                for c in range(CHUNKS):
                    pe.wait_ge(s_hid, b * CHUNKS + c + 1)
                    back, last_c = previous(ZSLOT, c)
                    for half in range(J // BANK):
                        if not (first and back):
                            pe.wait_ge(s_acc, (b - back) * P + last_c * J + (half + 1) * BANK)
                        z = bank[2 * ZSLOT[c] + half]
                        nc.tensor.matmul(z[:, :], ones16[:, :], bias16[:, 1, :, :], start=True, stop=False,
                                         skip_group_check=True)
                        for m in range(BANK):
                            last = nc.tensor.matmul(z[:, m * P:(m + 1) * P], hid[:, c % HR, half * BANK + m, :],
                                                    w2c[:, :], start=False, stop=(m == BANK - 1),
                                                    skip_group_check=True)
                        last.then_inc(s_z, 1)

            edge_graph(0, True)
            with pe.Fori(1, GRAPHS) as b:
                edge_graph(b, False)

        @block.scalar
        def _(act):
            def copy_bank(dst, k):
                return nc.scalar.activation(dst, graphs_of(k), ACT.Copy)

            act.wait_ge(s_wT, 1)
            nc.scalar.activation(w0T[:, :, :], bank[0][:, 0:2 * P].rearrange("p (t n) -> p t n", t=2), ACT.Copy)\
                .then_inc(s_set, 1)

            def l0_xT(q):
                act.wait_ge(s_xt, q + 1)
                act.wait_ge(s_xp, q)
                copy_bank(xT[:, :, :], 0).then_inc(s_xte, 1)

            def l0_proj(q):
                act.wait_ge(s_xp, q + 1)
                act.wait_ge(s_ag, q)
                copy_bank(proj[:, :, :], 2).then_inc(s_pe, 1)

            def l0_x1T(q):
                act.wait_ge(s_x1t, q + 1)
                act.wait_ge(s_h, q)
                copy_bank(x1T[:, :, :], 0).then_inc(s_x1e, 1)

            def l1_h(q):
                act.wait_ge(s_h, q + 1)
                act.wait_ge(s_att, q)
                nc.scalar.activation(src[:, :], bank[5][:, 0:2 * G].rearrange("p (g t) -> p g t", t=2)[:, :, 0],
                                     ACT.Copy).then_inc(s_src, 1)
                act.wait_ge(s_mh, q)
                copy_bank(h1[:, :, :], 3).then_inc(s_he, 1)

            def l1_exp(q):
                act.wait_ge(s_nm, q + 1)
                for g in range(G):
                    last = nc.scalar.activation(att[:, g, :], att[:, g, :], ACT.Exp, bias=soft[:, 1, g:g + 1],
                                                accum_out=soft[:, 2, g:g + 1])
                last.then_inc(s_ex, 1)

            def l1_attT(q):
                act.wait_ge(s_at, q + 1)
                act.wait_ge(s_mh, q)
                copy_bank(attT[:, :, :], 4).then_inc(s_ate, 1)

            def l1_relu(q):
                act.wait_ge(s_mh, q + 1)
                act.wait_ge(s_x2t, q)
                nc.scalar.activation(y1[:, :, :], graphs_of(3), ACT.Relu, scale=1.0 - SLOPE).then_inc(s_rl, 1)

            def l1_x2T(q):
                act.wait_ge(s_x2t, q + 1)
                act.wait_ge(s_su, q)
                copy_bank(x2T[:, :, :], 5).then_inc(s_x2e, 1)

            def l2_adjT(q):
                act.wait_ge(s_tr, q + 1)
                act.wait_ge(s_cv, q)
                copy_bank(adjT[:, :, :], 6).then_inc(s_tre, 1)

            def l2_support(q):
                act.wait_ge(s_su, q + 1)
                act.wait_ge(s_dis, q + 1)
                act.wait_ge(s_d2, 2 * q)
                for g in range(G):
                    last = nc.scalar.activation(supp[:, g, :], bank[7][:, g * P:(g + 1) * P], ACT.Copy,
                                                scale=dis[:, bass.ds(q * G + g, 1)])
                last.then_inc(s_sue, 1)

            def l2_x3T(q):
                act.wait_ge(s_x3t, q + 1)
                act.wait_ge(s_ab, q)
                copy_bank(x3T[:, :, :], 7).then_inc(s_x3e, 1)

            def l3_inputs(q):
                act.wait_ge(s_ab, q + 1)
                nc.scalar.activation(cols(aT_all, q), graphs_of(6), ACT.Identity, bias=e_b1_sb[:, 0:1])
                copy_bank(cols(bT_all, q), 7).then_inc(s_abe, 1)

            def layers(t, l0, l1, l2):
                if l2: l2_adjT(t - 2)
                if l0: l0_xT(t)
                if l1: l1_h(t - 1)
                if l2: l2_support(t - 2)
                if l0: l0_proj(t)
                if l1: l1_exp(t - 1)
                if l1: l1_attT(t - 1)
                if l1: l1_relu(t - 1)
                if l2: l2_x3T(t - 2)
                if l2: l3_inputs(t - 2)
                if l0: l0_x1T(t)
                if l1: l1_x2T(t - 1)

            layers(0, True, False, False)
            layers(1, True, True, False)
            with act.Fori(2, GROUPS) as t:
                layers(t, True, True, True)
            layers(GROUPS, False, True, True)
            layers(GROUPS + 1, False, False, True)

            def relu(g, c):
                act.wait_ge(s_pre, g + 1)
                nc.scalar.activation(hid[:, c % HR, :, :], hid[:, c % HR, :, :], ACT.Relu).then_inc(s_hid, 1)

            def squares(g, c):
                slot = c % 2
                act.wait_ge(s_z, 2 * g + 1)
                z = bank[2 * ZSLOT[c]][:, :].rearrange("p (m l) -> p m l", m=BANK)
                nc.scalar.activation(sq[:, slot, :, :], z[:, 0:WIDE, :], ACT.Square).then_inc(s_sq, 1)
                for m in range(WIDE, J):
                    if m == BANK:
                        act.wait_ge(s_z, 2 * g + 2)
                    z = bank[2 * ZSLOT[c] + m // BANK][:, (m % BANK) * P:(m % BANK + 1) * P]
                    last = nc.scalar.activation(junk[:, m - WIDE, :], z, ACT.Square, accum_out=ss[:, slot, m:m + 1])
                last.then_inc(s_ac, 1)

            def deviation(g, c):
                slot = c % 2
                act.wait_ge(s_red, g + 1)
                act.wait_ge(s_ac, g + 1)
                nc.scalar.activation(sd[:, slot, :], ss[:, slot, :], ACT.Sqrt, bias=eps_c[:, 0:1], scale=1.0 / P)\
                    .then_inc(s_sd, 1)

            def finish_deviation(b):
                act.wait_ge(s_fin, 5 * b + 5)
                nc.scalar.activation(fsd[:, 0:1], fmv[:, 1:2], ACT.Sqrt, bias=eps_c[:, 0:1]).then_inc(s_fsd, 1)

            def edge_graph(b, first, last):
                for c in range(CHUNKS):
                    g = b * CHUNKS + c
                    squares(g, c)
                    if not (last and c + AHEAD >= CHUNKS):
                        relu(g + AHEAD, c + AHEAD)
                    deviation(g, c)
                    if c == 7 and not first:
                        finish_deviation(b - 1)

            for c in range(AHEAD):
                relu(c, c)
            edge_graph(0, True, False)
            with act.Fori(1, GRAPHS - 1) as b:
                edge_graph(b, False, False)
            edge_graph(GRAPHS - 1, False, True)
            finish_deviation(GRAPHS - 1)

        @block.gpsimd
        def _(pool):
            nc.gpsimd.memset(ident[:, :], 0.0).then_inc(s_set, 1)
            nc.gpsimd.memset(half_c[:, :], -0.5).then_inc(s_set, 1)
            nc.gpsimd.memset(eps_c[:, :], EPS).then_inc(s_set, 1)
            nc.gpsimd.memset(ones16[:, :], 1.0).then_inc(s_set, 1)
            nc.gpsimd.memset(bias16[:, :, :, :], 0.0).then_inc(s_set, 1)
            pool.wait_ge(s_set, 5)
            nc.gpsimd.affine_select(out=ident[:, :], in_=ident[:, :], compare_op=ALU.not_equal, fill=1.0,
                                    base=0, pattern=[[-1, P]], channel_multiplier=1).then_inc(s_cst, 1)

            def rsqrt(k, q):
                pool.wait_ge(s_ve[k], q + 1)
                nc.gpsimd.tensor_tensor(lnrs[k][:, :], lnve[k][:, :], half_c[:, :], ALU.pow).then_inc(s_rs[k], 1)

            def degree(q):
                pool.wait_ge(s_ds, q + 1)
                nc.gpsimd.tensor_tensor(dtmp[:, 2, :], dtmp[:, 1, :], half_c[:, :], ALU.pow).then_inc(s_dp, 1)

            def l1_residual(q):
                pool.wait_ge(s_rl, q + 1)
                pool.wait_ge(s_x1k, q + 1)
                nc.gpsimd.tensor_tensor(y1[:, :, :], y1[:, :, :], cols(x_all, q), ALU.add).then_inc(s_xr, 1)

            def l2_bias(q):
                pool.wait_ge(s_x2k, q + 1)
                pool.wait_ge(s_d2, 2 * q)
                nc.gpsimd.tensor_tensor(x2b[:, :, :], cols(x_all, q),
                                        b2B[:, :].unsqueeze(1).to_broadcast([P, G, P]), ALU.add).then_inc(s_xb, 1)

            pool.wait_ge(s_wready, 1)

            def layers(t, l0, l1, l2):
                if l2: l2_bias(t - 2)
                if l0: degree(t)
                if l1: l1_residual(t - 1)
                if l2: rsqrt(2, t - 2)
                if l0: rsqrt(0, t)
                if l1: rsqrt(1, t - 1)

            layers(0, True, False, False)
            layers(1, True, True, False)
            with pool.Fori(2, GROUPS) as t:
                layers(t, True, True, True)
            layers(GROUPS, False, True, True)
            layers(GROUPS + 1, False, False, True)

            def sums(b, c, first):
                if not (first and c < HR):
                    pool.wait_ge(s_z, 2 * (b * CHUNKS + c - HR + 1))
                nc.gpsimd.tensor_tensor(hid[:, c % HR, :, :],
                                        aT_all[:, bass.ds(b, 1), :].to_broadcast([P, J, P]),
                                        bT_all[:, bass.ds(b, 1), c * J:(c + 1) * J].rearrange("p g j -> p (g j)")
                                        .unsqueeze(2).to_broadcast([P, J, P]), ALU.add).then_inc(s_pre, 1)

            pool.wait_ge(s_abe, GROUPS)
            for c in range(CHUNKS):
                sums(0, c, True)
            with pool.Fori(1, GRAPHS) as b:
                for c in range(CHUNKS):
                    sums(b, c, False)

        @block.vector
        def _(dve):
            steps = [0]
            s_v = sem("vector_setup")

            def step(ins):
                steps[0] += 1
                ins.then_inc(s_v, 1)
                dve.wait_ge(s_v, steps[0])

            dve.wait_ge(s_w, 16 * 12)
            dve.wait_ge(s_cst, 1)
            step(nc.vector.memset(carrier[:, :], 0.0))
            for t in range(2):
                step(nc.vector.tensor_tensor_reduce(junk[:, 0, :], w1_sb[:, :], a1B[:, t * P:(t + 1) * P], 1.0, 0.0,
                                                    ALU.mult, ALU.add, u[:, t:t + 1]))
            step(nc.vector.tensor_copy(u_dstB[:, :], u[:, 1:2].to_broadcast([P, P])))
            step(nc.vector.tensor_reduce(mean_c[:, 0:1], e_w2_sb[:, :], AX.X, ALU.add))
            step(nc.vector.tensor_reduce(mean_c[:, 1:2], rowB[:, 1, :], AX.X, ALU.add))
            step(nc.vector.tensor_scalar(mean_c[:, :], mean_c[:, :], 1.0 / P, None, ALU.mult))
            step(nc.vector.tensor_scalar(w2c[:, :], e_w2_sb[:, :], mean_c[:, 0:1], None, ALU.subtract))
            step(nc.vector.tensor_scalar(rowB[:, 1, :], rowB[:, 1, :], mean_c[:, 1:2], None, ALU.subtract))
            rest = rowB
            for k in range(3):
                step(nc.vector.tensor_copy(rowH[:, k, :, :], rest[:, :, :]))
                step(nc.vector.tensor_tensor(rowT[:, :, :], rest[:, :, :], rowH[:, k, :, :], ALU.subtract))
                rest = rowT
                row = slice(32 * k, 32 * k + 1)
                for t in range(2):
                    step(nc.vector.tensor_copy(bias16[row, t, :, :],
                                               rowH[row, k, t, :].unsqueeze(1).to_broadcast([1, BANK, P])))
            dve.wait_ge(s_set, 6)
            step(nc.vector.tensor_copy(mean_c[:, :], u[:, :]))
            nc.vector.tensor_copy(mean_c[:, :], u[:, :]).then_inc(s_wready, 1)

            def norm_stats(k, y, q):
                for g in range(G):
                    last = nc.vector.bn_stats(lnst[k][:, g, :], y[:, g, :])
                last.then_inc(s_ln[k], 1)
                wait_apart(s_ln[k], 2 * q + 1)
                for g in range(G):
                    last = nc.vector.bn_aggr(lnmv[k][:, g, :], lnst[k][:, g, :])
                last.then_inc(s_ln[k], 1)
                dve.wait_ge(s_ln[k], 2 * q + 2)
                nc.vector.tensor_scalar(lnve[k][:, :], lnmv[k][:, :, 1], EPS, None, ALU.add).then_inc(s_ve[k], 1)

            def wait_apart(s, count):
                dve.wait_ge(s, count)
                nc.vector.tensor_copy(carrier[:, 1:2], carrier[:, 0:1])

            s_ln = [sem(f"norm_step{k}") for k in range(3)]

            def normalise(k, y, q, done):
                dve.wait_ge(s_rs[k], q + 1)
                for g in range(G):
                    last = nc.vector.tensor_scalar(y[:, g, :], y[:, g, :], lnmv[k][:, g, 0:1], lnrs[k][:, g:g + 1],
                                                   ALU.subtract, ALU.mult)
                last.then_inc(done, 1)

            def l0_degree(q):
                dve.wait_ge(s_all, (q + 1) * 32)
                d = deg[:, bass.ds(q * G, G)]
                nc.vector.tensor_reduce(d, cols(adj_all, q), AX.X, ALU.add).then_inc(s_dg, 1)
                dve.wait_ge(s_dg, 3 * q + 1)
                nc.vector.tensor_scalar(dtmp[:, 0, :], d, 1.0, 0.0, ALU.add, ALU.is_equal).then_inc(s_dg, 1)
                nc.vector.reciprocal(rdeg[:, :], d)
                dve.wait_ge(s_dg, 3 * q + 2)
                nc.vector.scalar_tensor_tensor(out=dtmp[:, 1, :], in0=d, scalar=1.0, in1=dtmp[:, 0, :],
                                               op0=ALU.add, op1=ALU.add).then_inc(s_ds, 1)
                nc.vector.tensor_scalar(dtmp[:, 0, :], dtmp[:, 0, :], -1.0, 1.0, ALU.mult, ALU.add)\
                    .then_inc(s_dg, 1)

            s_dg = sem("degree_step")

            def l0_dis(q):
                dve.wait_ge(s_dp, q + 1)
                dve.wait_ge(s_dg, 3 * q + 3)
                nc.vector.tensor_tensor(dis[:, bass.ds(q * G, G)], dtmp[:, 2, :], dtmp[:, 0, :], ALU.mult)\
                    .then_inc(s_dis, 1)

            def l0_sum(q):
                dve.wait_ge(s_ag, q + 1)
                dve.wait_ge(s_x1t, q)
                nc.vector.tensor_tensor(y0[:, :, :], graphs_of(2), per_graph(rdeg), ALU.mult).then_inc(s_d0, 1)
                dve.wait_ge(s_d0, 3 * q + 1)
                nc.vector.tensor_tensor(y0[:, :, :], graphs_of(1), y0[:, :, :], ALU.add).then_inc(s_d0, 1)
                dve.wait_ge(s_d0, 3 * q + 2)
                nc.vector.scalar_tensor_tensor(out=y0[:, :, :], in0=y0[:, :, :], scalar=0.0, in1=cols(x_all, q),
                                               op0=ALU.max, op1=ALU.add).then_inc(s_d0, 1)
                dve.wait_ge(s_d0, 3 * q + 3)
                norm_stats(0, y0, q)

            def l0_norm(q):
                normalise(0, y0, q, s_x1)
                wait_apart(s_x1, q + 1)
                nc.vector.tensor_copy(cols(x_all, q), y0[:, :, :]).then_inc(s_x1k, 1)

            def l1_scores(q):
                dve.wait_ge(s_h, q + 1)
                dve.wait_ge(s_src, q + 1)
                dve.wait_ge(s_at, q)
                nc.vector.tensor_reduce(soft[:, 0, :], graphs_of(4), AX.X, ALU.max).then_inc(s_sf, 1)
                nc.vector.tensor_tensor(att[:, :, :], graphs_of(4), per_graph(src), ALU.add).then_inc(s_sf, 1)
                dve.wait_ge(s_sf, 4 * q + 1)
                nc.vector.scalar_tensor_tensor(out=soft[:, 3, :], in0=src[:, :], scalar=-1.0, in1=soft[:, 0, :],
                                               op0=ALU.mult, op1=ALU.subtract).then_inc(s_sf, 1)
                dve.wait_ge(s_sf, 4 * q + 3)
                nc.vector.scalar_tensor_tensor(out=soft[:, 1, :], in0=soft[:, 3, :], scalar=SLOPE, in1=soft[:, 3, :],
                                               op0=ALU.mult, op1=ALU.min).then_inc(s_sf, 1)
                dve.wait_ge(s_sf, 4 * q + 4)
                nc.vector.scalar_tensor_tensor(out=att[:, :, :], in0=att[:, :, :], scalar=SLOPE, in1=att[:, :, :],
                                               op0=ALU.mult, op1=ALU.max).then_inc(s_nm, 1)

            s_sf = sem("softmax_step")
            s_rd = sem("denominator_inverted")

            def l1_attention(q):
                dve.wait_ge(s_ex, q + 1)
                nc.vector.reciprocal(soft[:, 4, :], soft[:, 2, :]).then_inc(s_rd, 1)
                dve.wait_ge(s_rd, q + 1)
                for g in range(G):
                    last = nc.vector.scalar_tensor_tensor(
                        out=att[:, g, :], in0=att[:, g, :], scalar=soft[:, 4, g:g + 1],
                        in1=adj_all[:, bass.ds(q * G + g, 1), :].rearrange("p g n -> p (g n)"),
                        op0=ALU.mult, op1=ALU.add)
                last.then_inc(s_att, 1)

            def l1_sum(q):
                dve.wait_ge(s_xr, q + 1)
                nc.vector.scalar_tensor_tensor(out=y1[:, :, :], in0=graphs_of(3), scalar=SLOPE, in1=y1[:, :, :],
                                               op0=ALU.mult, op1=ALU.add).then_inc(s_d1, 1)
                dve.wait_ge(s_d1, q + 1)
                norm_stats(1, y1, q)

            def l1_norm(q):
                normalise(1, y1, q, s_x2)
                wait_apart(s_x2, q + 1)
                nc.vector.tensor_copy(cols(x_all, q), y1[:, :, :]).then_inc(s_x2k, 1)

            def l2_sum(q):
                dve.wait_ge(s_cv, q + 1)
                dve.wait_ge(s_x3t, q)
                dve.wait_ge(s_x3b, q)
                nc.vector.tensor_tensor(y2[:, :, :], graphs_of(6), supp[:, :, :], ALU.add).then_inc(s_d2, 1)
                dve.wait_ge(s_d2, 2 * q + 1)
                dve.wait_ge(s_xb, q + 1)
                for g in range(G):
                    last = nc.vector.scalar_tensor_tensor(out=y2[:, g, :], in0=y2[:, g, :],
                                                          scalar=dis[:, bass.ds(q * G + g, 1)], in1=x2b[:, g, :],
                                                          op0=ALU.mult, op1=ALU.add)
                last.then_inc(s_d2, 1)
                dve.wait_ge(s_d2, 2 * q + 2)
                norm_stats(2, y2, q)

            def l2_norm(q):
                normalise(2, y2, q, s_x3)
                dve.wait_ge(s_x3, q + 1)
                for g in range(G):
                    last = nc.vector.scalar_tensor_tensor(
                        out=x_all[:, bass.ds(q * G + g, 1), :].rearrange("p g n -> p (g n)"), in0=betaB[:, :],
                        scalar=deg[:, bass.ds(q * G + g, 1)], in1=y2[:, g, :], op0=ALU.mult, op1=ALU.add)
                last.then_inc(s_x3b, 1)

            def layers(t, l0, l1, l2):
                if l0: l0_degree(t)
                if l1: l1_scores(t - 1)
                if l0: l0_dis(t)
                if l1: l1_attention(t - 1)
                if l2: l2_sum(t - 2)
                if l0: l0_sum(t)
                if l2: l2_norm(t - 2)
                if l1: l1_sum(t - 1)
                if l0: l0_norm(t)
                if l1: l1_norm(t - 1)

            layers(0, True, False, False)
            layers(1, True, True, False)
            with dve.Fori(2, GROUPS) as t:
                layers(t, True, True, True)
            layers(GROUPS, False, True, True)
            layers(GROUPS + 1, False, False, True)

            def reduce(g, c):
                slot = c % 2
                dve.wait_ge(s_sq, g + 1)
                nc.vector.tensor_reduce(ss[:, slot, 0:WIDE], sq[:, slot, :, :], AX.X, ALU.add).then_inc(s_red, 1)

            def finish(b, k):
                if k == 0:
                    dve.wait_ge(s_acc, (b + 1) * P)
                    nc.vector.tensor_tensor(fin[:, 0, :], acc[:, 0, :], acc[:, 1, :], ALU.add).then_inc(s_fin, 1)
                if k == 1:
                    dve.wait_ge(s_fin, 5 * b + 1)
                    nc.vector.tensor_tensor(fin[:, 1, :], fin[:, 0, :], gammaB[:, :], ALU.mult).then_inc(s_fin, 1)
                if k == 2:
                    dve.wait_ge(s_fin, 5 * b + 2)
                    nc.vector.tensor_tensor(fin[:, 2, :], fin[:, 1, :],
                                            x_all[:, bass.ds(b, 1), :].rearrange("p g n -> p (g n)"), ALU.add)\
                        .then_inc(s_fin, 1)
                if k == 3:
                    dve.wait_ge(s_fin, 5 * b + 3)
                    nc.vector.bn_stats(fst[:, :], fin[:, 2, :]).then_inc(s_fin, 1)
                if k == 4:
                    wait_apart(s_fin, 5 * b + 4)
                    nc.vector.bn_aggr(fmv[:, :], fst[:, :]).then_inc(s_fin, 1)
                if k == 5:
                    dve.wait_ge(s_fsd, b + 1)
                    nc.vector.reciprocal(fsd[:, 1:2], fsd[:, 0:1]).then_inc(s_frd, 1)
                if k == 6:
                    dve.wait_ge(s_frd, b + 1)
                    dve.wait_ge(s_out, 16 * b)
                    nc.vector.tensor_scalar(res[:, :], fin[:, 2, :], fmv[:, 0:1], fsd[:, 1:2],
                                            ALU.subtract, ALU.mult).then_inc(s_res, 1)

            s_frd = sem("finish_inverted")
            FINISH = {0: 0, 1: 1, 2: 2, 3: 3, 4: 4, 9: 5, 10: 6}

            def edge_graph(b, first, last):
                for c in range(CHUNKS):
                    g = b * CHUNKS + c
                    slot = c % 2
                    dve.wait_ge(s_sd, g + 1)
                    nc.vector.reciprocal(rs[:, slot, :], sd[:, slot, :]).then_inc(s_wk, 1)
                    if c in FINISH and not first:
                        finish(b - 1, FINISH[c])
                    if not (last and c == CHUNKS - 1):
                        reduce(g + 1, c + 1)
                    dve.wait_ge(s_wk, 2 * g + 1)
                    nc.vector.tensor_tensor(wt[:, slot, :], rs[:, slot, :],
                                            adj_all[:, bass.ds(b, 1), c * J:(c + 1) * J].rearrange("p g j -> p (g j)"),
                                            ALU.mult).then_inc(s_wk, 1)
                    dve.wait_ge(s_wk, 2 * g + 2)
                    for m in range(J):
                        z = bank[2 * ZSLOT[c] + m // BANK][:, (m % BANK) * P:(m % BANK + 1) * P]
                        a = acc[:, m % 2, :]
                        if c == 0 and m < 2:
                            nc.vector.tensor_scalar(a, z, wt[:, slot, m:m + 1], None, ALU.mult).then_inc(s_acc, 1)
                        else:
                            dve.wait_ge(s_acc, b * P + c * J + m - 1)
                            nc.vector.scalar_tensor_tensor(out=a, in0=z, scalar=wt[:, slot, m:m + 1], in1=a,
                                                           op0=ALU.mult, op1=ALU.add).then_inc(s_acc, 1)

            reduce(0, 0)
            edge_graph(0, True, False)
            with dve.Fori(1, GRAPHS - 1) as b:
                edge_graph(b, False, False)
            edge_graph(GRAPHS - 1, False, True)
            for k in range(7):
                finish(GRAPHS - 1, k)


_INS = ['x', 'adj', 'L0_gnn_W', 'L0_gnn_b', 'L1_gnn_W', 'L1_gnn_a', 'L2_gnn_weight', 'L2_gnn_bias', 'L3_gnn_W1',
        'L3_gnn_b1', 'L3_gnn_W2', 'L3_gnn_b2', 'L3_gnn_gamma', 'L3_gnn_beta']
_OUTS = [((64, 128, 128), 'float32')]


def kernel(**inputs):
    import numpy as _np
    import concourse.bacc as _bacc
    from concourse import mybir as _mybir
    from concourse.bass_utils import run_bass_kernel_spmd as _run

    nc = _bacc.Bacc("TRN2", target_bir_lowering=False, num_devices=1)
    arrays, args = {}, []
    for name in _INS:
        a = _np.ascontiguousarray(inputs[name])
        arrays[f"in_{name}_dram"] = a
        args.append(nc.dram_tensor(f"in_{name}_dram", a.shape, _mybir.dt.from_np(a.dtype), kind="ExternalInput").ap())
    for i, (shape, dtype) in enumerate(_OUTS):
        dt = _mybir.dt.from_np(_np.dtype(dtype))
        args.append(nc.dram_tensor(f"out_{i}_dram", shape, dt, kind="ExternalOutput").ap())
    graph_layers_kernel(nc, *args)
    r = _run(nc, [arrays], core_ids=[0])
    return r.results[0]["out_0_dram"]
```

```python
from contextlib import ExitStack

import concourse.bass as bass
from concourse import mybir

F32 = mybir.dt.float32
BF16 = mybir.dt.bfloat16
ALU = mybir.AluOpType
ACT = mybir.ActivationFunctionType
AX = mybir.AxisListType

EPS = 1e-5
SLOPE = 0.2


def graph_layers_kernel(nc, x, adj, w0, b0, w1, a1, w2, b2, e_w1, e_b1, e_w2, e_b2, e_gamma, e_beta, out):
    GRAPHS, N, D = x.shape
    P = 128
    assert N == P and D == P
    G = 4
    GROUPS = GRAPHS // G
    GW = G * P
    J = 16
    CHUNKS = P // J
    BANK = 4
    BANKS = J // BANK
    PIECE = 8
    PIECES = P // PIECE
    PER = J // PIECE
    WIDE = 8
    REDUCE_AT = 10
    INVERT_AT = 12
    WEIGH_AT = 14
    HR = 4
    AHEAD = 2

    with ExitStack() as ctx:
        def sb(name, shape, dt=F32):
            return ctx.enter_context(nc.sbuf_tensor(name, shape, dt))

        def sem(name):
            return ctx.enter_context(nc.semaphore(name))

        adj_all = sb("adj_all", [P, GRAPHS, P])
        x_all = sb("x_all", [P, GRAPHS, P])
        aT_all = sb("aT_all", [P, GRAPHS, P])
        bT_all = sb("bT_all", [P, GRAPHS, P])
        ident = sb("ident", [P, P])
        ones16 = sb("ones16", [P, P], BF16)
        w0_sb = sb("w0_sb", [P, 2 * P])
        w0T = sb("w0T", [P, 2, P])
        w1_sb = sb("w1_sb", [P, P])
        a1B = sb("a1B", [P, 2 * P])
        u = sb("u", [P, 2])
        u_dstB = sb("u_dstB", [P, P])
        w2_sb = sb("w2_sb", [P, P])
        b2B = sb("b2B", [P, P])
        e_w1_sb = sb("e_w1_sb", [P, 2, P])
        e_b1_sb = sb("e_b1_sb", [P, 1])
        e_w2_sb = sb("e_w2_sb", [P, P])
        w2c = sb("w2c", [P, P])
        rowB = sb("rowB", [P, 2, P])
        rowH = sb("rowH", [P, 3, 2, P], BF16)
        bias16 = sb("bias16", [P, 2, BANK, P], BF16)
        gammaB = sb("gammaB", [P, P])
        betaB = sb("betaB", [P, P])
        mean_c = sb("mean_c", [P, 2])
        eps_c = sb("eps_c", [P, 1])
        half_c = sb("half_c", [P, G])
        xq = sb("xq", [P, G, P])
        adjq = sb("adjq", [P, G, P])
        xT = sb("xT", [P, G, P])
        proj = sb("proj", [P, G, P])
        y0 = sb("y0", [P, G, P])
        x1T = sb("x1T", [P, G, P])
        h1 = sb("h1", [P, G, P])
        att = sb("att", [P, G, P])
        attT = sb("attT", [P, G, P])
        y1 = sb("y1", [P, G, P])
        x2T = sb("x2T", [P, G, P])
        adjr = sb("adjr", [P, G, P])
        adjT = sb("adjT", [P, G, P])
        supp = sb("supp", [P, G, P])
        y2 = sb("y2", [P, G, P])
        x2b = sb("x2b", [P, G, P])
        x3T = sb("x3T", [P, G, P])
        deg = sb("deg", [P, GRAPHS])
        rdeg = sb("rdeg", [P, G])
        dis = sb("dis", [P, GRAPHS])
        dtmp = sb("dtmp", [P, 3, G])
        src = sb("src", [P, G])
        soft = sb("soft", [P, 5, G])
        lnst = [sb(f"lnst{k}", [P, G, 6]) for k in range(3)]
        lnmv = [sb(f"lnmv{k}", [P, G, 2]) for k in range(3)]
        lnve = [sb(f"lnve{k}", [P, G]) for k in range(3)]
        lnrs = [sb(f"lnrs{k}", [P, G]) for k in range(3)]
        hid = sb("hid", [P, HR, PIECE, P])
        sq = sb("sq", [P, 2, WIDE, P])
        junk = sb("junk", [P, J - WIDE, P])
        ss = sb("ss", [P, 2, J])
        sd = sb("sd", [P, 2, J])
        rs = sb("rs", [P, 2, J])
        wt = sb("wt", [P, 2, J])
        acc = sb("acc", [P, 2, P])
        fin = sb("fin", [P, 3, P])
        carrier = sb("carrier", [P, 2])
        fst = sb("fst", [P, 6])
        fmv = sb("fmv", [P, 2])
        fsd = sb("fsd", [P, 2])

        psum = ctx.enter_context(nc.psum_tensor("psum", [P, 8, 512], F32))
        bank = [psum[:, k, :] for k in range(8)]

        def z_of(c, m, n=1):
            at = (c % 2) * J + m
            return psum[:, :, :].rearrange("p k n -> p (k n)")[:, at * P:(at + n) * P]

        def graphs_of(k):
            return bank[k][:, :].rearrange("p (g n) -> p g n", g=G)

        def per_graph(t):
            return t[:, :].unsqueeze(2).to_broadcast([P, G, P])

        s_w = sem("weights_loaded")
        s_cst = sem("constants_set")
        s_wT = sem("w0_transposed")
        s_set = sem("setup_step")
        s_wready = sem("weights_ready")
        s_xq = sem("x_group_loaded")
        s_aq = sem("adj_group_loaded")
        s_r = sem("adj_again_loaded")
        s_all = sem("kept_inputs_loaded")
        s_xt = sem("xT_in_psum")
        s_xte = sem("xT_ready")
        s_xp = sem("self_and_neighbour_products")
        s_pe = sem("proj_ready")
        s_ag = sem("aggregated_in_psum")
        s_d0 = sem("vector_L0_step")
        s_rs = [sem(f"rsqrt_ready{k}") for k in range(3)]
        s_ve = [sem(f"variance_ready{k}") for k in range(3)]
        s_ds = sem("degree_shifted")
        s_dp = sem("degree_power")
        s_dis = sem("dis_ready")
        s_x1 = sem("x1_ready")
        s_x1k = sem("x1_kept")
        s_x1t = sem("x1T_in_psum")
        s_x1e = sem("x1T_ready")
        s_h = sem("h_and_scores_in_psum")
        s_he = sem("h_ready")
        s_src = sem("src_score_ready")
        s_d1 = sem("vector_L1_step")
        s_nm = sem("scores_ready")
        s_ex = sem("exp_ready")
        s_att = sem("attention_ready")
        s_at = sem("attention_T_in_psum")
        s_ate = sem("attention_T_ready")
        s_mh = sem("attended_in_psum")
        s_rl = sem("attended_relu_ready")
        s_xr = sem("x1_plus_relu_ready")
        s_x2 = sem("x2_ready")
        s_x2k = sem("x2_kept")
        s_x2t = sem("x2T_in_psum")
        s_x2e = sem("x2T_ready")
        s_tr = sem("adjT_in_psum")
        s_tre = sem("adjT_ready")
        s_su = sem("support_in_psum")
        s_sue = sem("support_ready")
        s_xb = sem("x2_plus_bias_ready")
        s_cv = sem("convolved_in_psum")
        s_d2 = sem("vector_L2_step")
        s_x3 = sem("x3_ready")
        s_x3t = sem("x3T_in_psum")
        s_x3e = sem("x3T_ready")
        s_ab = sem("a_and_b_in_psum")
        s_abe = sem("a_and_b_ready")
        s_x3b = sem("residual_ready")
        s_bt = sem("beta_times_degree")
        s_pre = sem("sums_ready")
        s_hid = sem("hidden_ready")
        s_z = sem("z_bank_ready")
        s_sq = sem("squares_ready")
        s_half = sem("squares_halved")
        s_red = sem("squares_summed")
        s_ac = sem("accumulated_squares")
        s_sd = sem("deviation_ready")
        s_inv = sem("deviation_inverted")
        s_wk = sem("weights_of_chunk_ready")
        s_acc = sem("z_accumulated")
        s_fin = sem("finish_step")
        s_gam = sem("scaled_and_residual_added")
        s_fsd = sem("finish_deviation")
        s_res = sem("result_ready")
        s_out = sem("result_stored")

        def cols(t, q):
            return t[:, bass.ds(q * G, G), :]

        block = ctx.enter_context(nc.Block())

        @block.sync
        def _(sp):
            def row(ap):
                return ap.rearrange("(a n) -> a n", a=1).to_broadcast([P, ap.shape[0]])

            for dst, s in ((w0_sb[:, :], w0), (w1_sb[:, :], w1), (w2_sb[:, :], w2),
                           (e_w1_sb[:, :, :], e_w1.rearrange("(t h) k -> h t k", t=2)),
                           (e_w2_sb[:, :], e_w2), (e_b1_sb[:, :], e_b1.rearrange("(k a) -> k a", a=1)),
                           (a1B[:, :], row(a1)), (b2B[:, :], row(b2)), (gammaB[:, :], row(e_gamma)),
                           (betaB[:, :], row(e_beta)), (rowB[:, 0, :], row(b0)), (rowB[:, 1, :], row(e_b2))):
                sp.dma_start(dst, s).then_inc(s_w, 16)

            def group(t, q):
                return t[bass.ds(q * G, G), :, :].rearrange("g n d -> n g d")

            def kept(q):
                sp.wait_ge(s_all, q * 32)
                sp.dma_start(cols(x_all, q), group(x, q)).then_inc(s_all, 16)
                sp.dma_start(cols(adj_all, q), group(adj, q)).then_inc(s_all, 16)

            def for_l0(q):
                sp.wait_ge(s_xq, q * 16)
                sp.wait_ge(s_xt, q)
                sp.dma_start(xq[:, :, :], group(x, q)).then_inc(s_xq, 16)
                sp.wait_ge(s_aq, q * 16)
                sp.wait_ge(s_ag, q)
                sp.dma_start(adjq[:, :, :], group(adj, q)).then_inc(s_aq, 16)

            def for_l2(q):
                sp.wait_ge(s_r, q * 16)
                sp.wait_ge(s_tr, q)
                sp.dma_start(adjr[:, :, :], group(adj, q)).then_inc(s_r, 16)

            for_l0(0)
            kept(0)
            kept(1)
            for_l0(1)
            for_l2(0)
            with sp.Fori(2, GROUPS) as q:
                kept(q)
                for_l0(q)
                for_l2(q - 1)
            for_l2(GROUPS - 1)
            with sp.Fori(0, GRAPHS) as b:
                sp.wait_ge(s_res, b + 1)
                sp.dma_start(out[bass.ds(b, 1), :, :].rearrange("g n d -> n g d"),
                             x_all[:, bass.ds(b, 1), :]).then_inc(s_out, 16)
            sp.wait_ge(s_out, 16 * GRAPHS)

        @block.tensor
        def _(pe):
            def transposes(k, source):
                for g in range(G):
                    last = nc.tensor.transpose(bank[k][:, g * P:(g + 1) * P], source[:, g, :], ident[:, :])
                return last

            pe.wait_ge(s_w, 16 * 12)
            pe.wait_ge(s_cst, 1)
            nc.tensor.transpose(bank[0][:, 0:P], w0_sb[:, 0:P], ident[:, :])
            nc.tensor.transpose(bank[0][:, P:2 * P], w0_sb[:, P:2 * P], ident[:, :]).then_inc(s_wT, 1)
            pe.wait_ge(s_wready, 1)

            def l0_transpose(q):
                pe.wait_ge(s_xq, (q + 1) * 16)
                pe.wait_ge(s_x1e, q)
                transposes(0, xq).then_inc(s_xt, 1)

            def l0_project(q):
                pe.wait_ge(s_xte, q + 1)
                pe.wait_ge(s_ve[0], q)
                nc.tensor.matmul(bank[1][:, :], ones16[:, :], bias16[:, 0, :, :], start=True, stop=False,
                                 skip_group_check=True)
                for g in range(G):
                    nc.tensor.matmul(bank[1][:, g * P:(g + 1) * P], xT[:, g, :], w0T[:, 0, :],
                                     start=False, stop=(g == G - 1), skip_group_check=True)
                for g in range(G):
                    last = nc.tensor.matmul(bank[2][:, g * P:(g + 1) * P], xT[:, g, :], w0T[:, 1, :],
                                            start=True, stop=True)
                last.then_inc(s_xp, 1)

            def l0_aggregate(q):
                pe.wait_ge(s_aq, (q + 1) * 16)
                pe.wait_ge(s_pe, q + 1)
                for g in range(G):
                    last = nc.tensor.matmul(bank[2][:, g * P:(g + 1) * P], adjq[:, g, :], proj[:, g, :],
                                            start=True, stop=True)
                last.then_inc(s_ag, 1)

            def l0_x1T(q):
                pe.wait_ge(s_x1, q + 1)
                transposes(0, y0).then_inc(s_x1t, 1)

            def l1_scores(q):
                pe.wait_ge(s_x1e, q + 1)
                pe.wait_ge(s_d1, q)
                for g in range(G):
                    nc.tensor.matmul(bank[3][:, g * P:(g + 1) * P], x1T[:, g, :], w1_sb[:, :], start=True, stop=True)
                pe.wait_ge(s_ate, q)
                nc.tensor.matmul(bank[4][:, :], u_dstB[:, :], x1T[:, :, :], start=True, stop=True)
                pe.wait_ge(s_x2e, q)
                for g in range(G):
                    last = nc.tensor.matmul(bank[5][:, 2 * g:2 * g + 2], x1T[:, g, :], u[:, 0:2],
                                            start=True, stop=True)
                last.then_inc(s_h, 1)

            def l1_transpose(q):
                pe.wait_ge(s_att, q + 1)
                transposes(4, att).then_inc(s_at, 1)

            def l1_attend(q):
                pe.wait_ge(s_ate, q + 1)
                pe.wait_ge(s_he, q + 1)
                for g in range(G):
                    last = nc.tensor.matmul(bank[3][:, g * P:(g + 1) * P], attT[:, g, :], h1[:, g, :],
                                            start=True, stop=True)
                last.then_inc(s_mh, 1)

            def l1_x2T(q):
                pe.wait_ge(s_x2, q + 1)
                transposes(5, y1).then_inc(s_x2t, 1)

            def l2_adjT(q):
                pe.wait_ge(s_r, (q + 1) * 16)
                pe.wait_ge(s_abe, q)
                transposes(6, adjr).then_inc(s_tr, 1)

            def l2_support(q):
                pe.wait_ge(s_x2e, q + 1)
                for g in range(G):
                    last = nc.tensor.matmul(bank[7][:, g * P:(g + 1) * P], x2T[:, g, :], w2_sb[:, :],
                                            start=True, stop=True)
                last.then_inc(s_su, 1)

            def l2_convolve(q):
                pe.wait_ge(s_tre, q + 1)
                pe.wait_ge(s_sue, q + 1)
                for g in range(G):
                    last = nc.tensor.matmul(bank[6][:, g * P:(g + 1) * P], adjT[:, g, :], supp[:, g, :],
                                            start=True, stop=True)
                last.then_inc(s_cv, 1)

            def l2_x3T(q):
                pe.wait_ge(s_x3, q + 1)
                transposes(7, y2).then_inc(s_x3t, 1)

            def l3_inputs(q):
                pe.wait_ge(s_x3e, q + 1)
                nc.tensor.matmul(bank[6][:, :], e_w1_sb[:, 0, :], x3T[:, :, :], start=True, stop=True)
                nc.tensor.matmul(bank[7][:, :], e_w1_sb[:, 1, :], x3T[:, :, :], start=True, stop=True)\
                    .then_inc(s_ab, 1)

            def layers(t, l0, l1, l2):
                if l2: l2_adjT(t - 2)
                if l0: l0_transpose(t)
                if l1: l1_scores(t - 1)
                if l2: l2_support(t - 2)
                if l0: l0_project(t)
                if l2: l2_convolve(t - 2)
                if l1: l1_transpose(t - 1)
                if l0: l0_aggregate(t)
                if l1: l1_attend(t - 1)
                if l2: l2_x3T(t - 2)
                if l2: l3_inputs(t - 2)
                if l0: l0_x1T(t)
                if l1: l1_x2T(t - 1)

            layers(0, True, False, False)
            layers(1, True, True, False)
            layers(2, True, True, True)
            with pe.Fori(3, GROUPS) as t:
                layers(t, True, True, True)
            layers(GROUPS, False, True, True)
            layers(GROUPS + 1, False, False, True)

            pe.wait_ge(s_abe, GROUPS)
            pe.wait_ge(s_ve[0], GROUPS)
            pe.wait_ge(s_d1, GROUPS)

            def edge_graph(b, first):
                for c in range(CHUNKS):
                    for k in range(BANKS):
                        piece = c * PER + k * BANK // PIECE
                        if k * BANK % PIECE == 0:
                            pe.wait_ge(s_hid, b * PIECES + piece + 1)
                        if not (first and c < 2):
                            pe.wait_ge(s_acc, b * P + (c - 2) * J + (k + 1) * BANK)
                        nc.tensor.matmul(z_of(c, k * BANK, BANK), ones16[:, :], bias16[:, 1, :, :],
                                         start=True, stop=False, skip_group_check=True)
                        for m in range(BANK):
                            last = nc.tensor.matmul(z_of(c, k * BANK + m),
                                                    hid[:, piece % HR, (k * BANK + m) % PIECE, :], w2c[:, :],
                                                    start=False, stop=(m == BANK - 1), skip_group_check=True)
                        last.then_inc(s_z, 1)

            edge_graph(0, True)
            with pe.Fori(1, GRAPHS) as b:
                edge_graph(b, False)

        @block.scalar
        def _(act):
            def copy_bank(dst, k):
                return nc.scalar.activation(dst, graphs_of(k), ACT.Copy)

            act.wait_ge(s_wT, 1)
            nc.scalar.activation(w0T[:, :, :], bank[0][:, 0:2 * P].rearrange("p (t n) -> p t n", t=2), ACT.Copy)\
                .then_inc(s_set, 1)

            def l0_xT(q):
                act.wait_ge(s_xt, q + 1)
                act.wait_ge(s_xp, q)
                copy_bank(xT[:, :, :], 0).then_inc(s_xte, 1)

            def l0_proj(q):
                act.wait_ge(s_xp, q + 1)
                act.wait_ge(s_ag, q)
                copy_bank(proj[:, :, :], 2).then_inc(s_pe, 1)

            def l0_x1T(q):
                act.wait_ge(s_x1t, q + 1)
                act.wait_ge(s_h, q)
                copy_bank(x1T[:, :, :], 0).then_inc(s_x1e, 1)

            def l1_h(q):
                act.wait_ge(s_h, q + 1)
                act.wait_ge(s_att, q)
                nc.scalar.activation(src[:, :], bank[5][:, 0:2 * G].rearrange("p (g t) -> p g t", t=2)[:, :, 0],
                                     ACT.Copy).then_inc(s_src, 1)
                act.wait_ge(s_mh, q)
                copy_bank(h1[:, :, :], 3).then_inc(s_he, 1)

            def l1_exp(q):
                act.wait_ge(s_nm, q + 1)
                for g in range(G):
                    last = nc.scalar.activation(att[:, g, :], att[:, g, :], ACT.Exp, bias=soft[:, 1, g:g + 1],
                                                accum_out=soft[:, 2, g:g + 1])
                last.then_inc(s_ex, 1)

            def l1_attT(q):
                act.wait_ge(s_at, q + 1)
                act.wait_ge(s_mh, q)
                copy_bank(attT[:, :, :], 4).then_inc(s_ate, 1)

            def l1_relu(q):
                act.wait_ge(s_mh, q + 1)
                act.wait_ge(s_x2t, q)
                nc.scalar.activation(y1[:, :, :], graphs_of(3), ACT.Relu, scale=1.0 - SLOPE).then_inc(s_rl, 1)

            def l1_x2T(q):
                act.wait_ge(s_x2t, q + 1)
                act.wait_ge(s_su, q)
                copy_bank(x2T[:, :, :], 5).then_inc(s_x2e, 1)

            def l2_adjT(q):
                act.wait_ge(s_tr, q + 1)
                act.wait_ge(s_cv, q)
                copy_bank(adjT[:, :, :], 6).then_inc(s_tre, 1)

            def l2_support(q):
                act.wait_ge(s_su, q + 1)
                act.wait_ge(s_dis, q + 1)
                act.wait_ge(s_d2, 2 * q)
                for g in range(G):
                    last = nc.scalar.activation(supp[:, g, :], bank[7][:, g * P:(g + 1) * P], ACT.Copy,
                                                scale=dis[:, bass.ds(q * G + g, 1)])
                last.then_inc(s_sue, 1)

            def l2_x3T(q):
                act.wait_ge(s_x3t, q + 1)
                act.wait_ge(s_ab, q)
                copy_bank(x3T[:, :, :], 7).then_inc(s_x3e, 1)

            def l3_inputs(q):
                act.wait_ge(s_ab, q + 1)
                nc.scalar.activation(cols(aT_all, q), graphs_of(6), ACT.Identity, bias=e_b1_sb[:, 0:1])
                copy_bank(cols(bT_all, q), 7).then_inc(s_abe, 1)

            def layers(t, l0, l1, l2):
                if l2: l2_adjT(t - 2)
                if l0: l0_xT(t)
                if l1: l1_h(t - 1)
                if l2: l2_support(t - 2)
                if l0: l0_proj(t)
                if l1: l1_exp(t - 1)
                if l1: l1_attT(t - 1)
                if l1: l1_relu(t - 1)
                if l2: l2_x3T(t - 2)
                if l2: l3_inputs(t - 2)
                if l0: l0_x1T(t)
                if l1: l1_x2T(t - 1)

            layers(0, True, False, False)
            layers(1, True, True, False)
            layers(2, True, True, True)
            with act.Fori(3, GROUPS) as t:
                layers(t, True, True, True)
            layers(GROUPS, False, True, True)
            layers(GROUPS + 1, False, False, True)

            def relu(n, h):
                act.wait_ge(s_pre, n + 1)
                nc.scalar.activation(hid[:, h % HR, :, :], hid[:, h % HR, :, :], ACT.Relu).then_inc(s_hid, 1)

            SPLIT = 8

            def squares(g, c, part):
                slot = c % 2
                if part == 0:
                    act.wait_ge(s_z, BANKS * g + (WIDE + BANK - 1) // BANK)
                    nc.scalar.activation(sq[:, slot, :, :], z_of(c, 0, WIDE).rearrange("p (m l) -> p m l", m=WIDE),
                                         ACT.Square).then_inc(s_sq, 1)
                for m in (range(WIDE, SPLIT), range(SPLIT, J))[part]:
                    if m % BANK == 0:
                        act.wait_ge(s_z, BANKS * g + m // BANK + 1)
                    last = nc.scalar.activation(junk[:, m - WIDE, :], z_of(c, m), ACT.Square,
                                                accum_out=ss[:, slot, m:m + 1])
                if part == 1:
                    last.then_inc(s_ac, 1)

            def deviation(g, c):
                slot = c % 2
                act.wait_ge(s_red, g + 1)
                act.wait_ge(s_ac, g + 1)
                nc.scalar.activation(sd[:, slot, :], ss[:, slot, :], ACT.Sqrt, bias=eps_c[:, 0:1], scale=1.0 / P)\
                    .then_inc(s_sd, 1)

            def finish_deviation(b):
                act.wait_ge(s_fin, 3 * b + 3)
                nc.scalar.activation(fsd[:, 0:1], fmv[:, 1:2], ACT.Sqrt, bias=eps_c[:, 0:1]).then_inc(s_fsd, 1)

            def edge_graph(b, first, last):
                for c in range(CHUNKS):
                    g = b * CHUNKS + c
                    for part in range(PER):
                        squares(g, c, part)
                        h = c * PER + part + AHEAD
                        if not (last and h >= PIECES):
                            relu(b * PIECES + h, h)
                    deviation(g, c)
                    if c == 5 and not first:
                        finish_deviation(b - 1)

            for c in range(AHEAD):
                relu(c, c)
            edge_graph(0, True, False)
            with act.Fori(1, GRAPHS - 1) as b:
                edge_graph(b, False, False)
            edge_graph(GRAPHS - 1, False, True)
            finish_deviation(GRAPHS - 1)

        @block.gpsimd
        def _(pool):
            nc.gpsimd.memset(ident[:, :], 0.0).then_inc(s_set, 1)
            nc.gpsimd.memset(half_c[:, :], -0.5).then_inc(s_set, 1)
            nc.gpsimd.memset(eps_c[:, :], EPS).then_inc(s_set, 1)
            nc.gpsimd.memset(ones16[:, :], 1.0).then_inc(s_set, 1)
            nc.gpsimd.memset(bias16[:, :, :, :], 0.0).then_inc(s_set, 1)
            pool.wait_ge(s_set, 5)
            nc.gpsimd.affine_select(out=ident[:, :], in_=ident[:, :], compare_op=ALU.not_equal, fill=1.0,
                                    base=0, pattern=[[-1, P]], channel_multiplier=1).then_inc(s_cst, 1)

            def rsqrt(k, q):
                pool.wait_ge(s_ve[k], q + 1)
                nc.gpsimd.tensor_tensor(lnrs[k][:, :], lnve[k][:, :], half_c[:, :], ALU.pow).then_inc(s_rs[k], 1)

            def degree(q):
                pool.wait_ge(s_ds, q + 1)
                nc.gpsimd.tensor_tensor(dtmp[:, 2, :], dtmp[:, 1, :], half_c[:, :], ALU.pow).then_inc(s_dp, 1)

            def l1_residual(q):
                pool.wait_ge(s_rl, q + 1)
                pool.wait_ge(s_x1k, q + 1)
                nc.gpsimd.tensor_tensor(y1[:, :, :], y1[:, :, :], cols(x_all, q), ALU.add).then_inc(s_xr, 1)

            def l2_bias(q):
                pool.wait_ge(s_x2k, q + 1)
                pool.wait_ge(s_d2, 2 * q)
                nc.gpsimd.tensor_tensor(x2b[:, :, :], cols(x_all, q),
                                        b2B[:, :].unsqueeze(1).to_broadcast([P, G, P]), ALU.add).then_inc(s_xb, 1)

            pool.wait_ge(s_wready, 1)

            def layers(t, l0, l1, l2):
                if l2: l2_bias(t - 2)
                if l0: degree(t)
                if l1: l1_residual(t - 1)
                if l2: rsqrt(2, t - 2)
                if l0: rsqrt(0, t)
                if l1: rsqrt(1, t - 1)

            layers(0, True, False, False)
            layers(1, True, True, False)
            layers(2, True, True, True)
            with pool.Fori(3, GROUPS) as t:
                layers(t, True, True, True)
            layers(GROUPS, False, True, True)
            layers(GROUPS + 1, False, False, True)

            def sums(b, h, first):
                if not (first and h < HR):
                    pool.wait_ge(s_z, (b * PIECES + h - HR + 1) * (PIECE // BANK))
                nc.gpsimd.tensor_tensor(hid[:, h % HR, :, :],
                                        aT_all[:, bass.ds(b, 1), :].to_broadcast([P, PIECE, P]),
                                        bT_all[:, bass.ds(b, 1), h * PIECE:(h + 1) * PIECE]
                                        .rearrange("p g j -> p (g j)").unsqueeze(2).to_broadcast([P, PIECE, P]),
                                        ALU.add).then_inc(s_pre, 1)

            def scale(b):
                pool.wait_ge(s_fin, 3 * b + 1)
                nc.gpsimd.tensor_tensor(fin[:, 1, :], fin[:, 0, :], gammaB[:, :], ALU.mult).then_inc(s_gam, 1)
                pool.wait_ge(s_gam, 2 * b + 1)
                nc.gpsimd.tensor_tensor(fin[:, 2, :], fin[:, 1, :],
                                        x_all[:, bass.ds(b, 1), :].rearrange("p g n -> p (g n)"), ALU.add)\
                    .then_inc(s_gam, 1)

            def halve(g, c):
                slot = c % 2
                pool.wait_ge(s_sq, g + 1)
                nc.gpsimd.tensor_tensor(sq[:, slot, :, 0:P // 2], sq[:, slot, :, 0:P // 2], sq[:, slot, :, P // 2:P],
                                        ALU.add).then_inc(s_half, 1)

            SCALE_AT = 6
            pool.wait_ge(s_abe, GROUPS)
            for h in range(PIECES):
                sums(0, h, True)
                if h >= HR and h % PER == 0:
                    halve((h - HR) // PER, (h - HR) // PER)
            with pool.Fori(1, GRAPHS) as b:
                for h in range(PIECES):
                    sums(b, h, False)
                    if h % PER == 0:
                        halve(b * CHUNKS + (h - HR) // PER, (h - HR) // PER)
                    if h == SCALE_AT:
                        scale(b - 1)
            for c in range(CHUNKS - HR // PER, CHUNKS):
                halve((GRAPHS - 1) * CHUNKS + c, c)
            scale(GRAPHS - 1)

        @block.vector
        def _(dve):
            steps = [0]
            s_v = sem("vector_setup")

            def step(ins):
                steps[0] += 1
                ins.then_inc(s_v, 1)
                dve.wait_ge(s_v, steps[0])

            dve.wait_ge(s_w, 16 * 12)
            dve.wait_ge(s_cst, 1)
            step(nc.vector.memset(carrier[:, :], 0.0))
            for t in range(2):
                step(nc.vector.tensor_tensor_reduce(junk[:, 0, :], w1_sb[:, :], a1B[:, t * P:(t + 1) * P], 1.0, 0.0,
                                                    ALU.mult, ALU.add, u[:, t:t + 1]))
            step(nc.vector.tensor_copy(u_dstB[:, :], u[:, 1:2].to_broadcast([P, P])))
            step(nc.vector.tensor_reduce(mean_c[:, 0:1], e_w2_sb[:, :], AX.X, ALU.add))
            step(nc.vector.tensor_reduce(mean_c[:, 1:2], rowB[:, 1, :], AX.X, ALU.add))
            step(nc.vector.tensor_scalar(mean_c[:, :], mean_c[:, :], 1.0 / P, None, ALU.mult))
            step(nc.vector.tensor_scalar(w2c[:, :], e_w2_sb[:, :], mean_c[:, 0:1], None, ALU.subtract))
            step(nc.vector.tensor_scalar(rowB[:, 1, :], rowB[:, 1, :], mean_c[:, 1:2], None, ALU.subtract))
            rest = rowB
            for k in range(3):
                step(nc.vector.tensor_copy(rowH[:, k, :, :], rest[:, :, :]))
                step(nc.vector.tensor_tensor(fin[:, 0:2, :], rest[:, :, :], rowH[:, k, :, :], ALU.subtract))
                rest = fin[:, 0:2, :]
                row = slice(32 * k, 32 * k + 1)
                for t in range(2):
                    step(nc.vector.tensor_copy(bias16[row, t, :, :],
                                               rowH[row, k, t, :].unsqueeze(1).to_broadcast([1, BANK, P])))
            dve.wait_ge(s_set, 6)
            step(nc.vector.tensor_copy(mean_c[:, :], u[:, :]))
            nc.vector.tensor_copy(mean_c[:, :], u[:, :]).then_inc(s_wready, 1)

            def norm_stats(k, y, q):
                for g in range(G):
                    last = nc.vector.bn_stats(lnst[k][:, g, :], y[:, g, :])
                last.then_inc(s_ln[k], 1)
                wait_apart(s_ln[k], 2 * q + 1)
                for g in range(G):
                    last = nc.vector.bn_aggr(lnmv[k][:, g, :], lnst[k][:, g, :])
                last.then_inc(s_ln[k], 1)
                dve.wait_ge(s_ln[k], 2 * q + 2)
                nc.vector.tensor_scalar(lnve[k][:, :], lnmv[k][:, :, 1], EPS, None, ALU.add).then_inc(s_ve[k], 1)

            def wait_apart(s, count):
                dve.wait_ge(s, count)
                nc.vector.tensor_copy(carrier[:, 1:2], carrier[:, 0:1])

            s_ln = [sem(f"norm_step{k}") for k in range(3)]

            def normalise(k, y, q, done):
                dve.wait_ge(s_rs[k], q + 1)
                for g in range(G):
                    last = nc.vector.tensor_scalar(y[:, g, :], y[:, g, :], lnmv[k][:, g, 0:1], lnrs[k][:, g:g + 1],
                                                   ALU.subtract, ALU.mult)
                last.then_inc(done, 1)

            def l0_degree(q):
                dve.wait_ge(s_all, (q + 1) * 32)
                d = deg[:, bass.ds(q * G, G)]
                nc.vector.tensor_reduce(d, cols(adj_all, q), AX.X, ALU.add).then_inc(s_dg, 1)
                dve.wait_ge(s_dg, 3 * q + 1)
                nc.vector.tensor_scalar(dtmp[:, 0, :], d, 1.0, 0.0, ALU.add, ALU.is_equal).then_inc(s_dg, 1)
                nc.vector.reciprocal(rdeg[:, :], d)
                dve.wait_ge(s_dg, 3 * q + 2)
                nc.vector.scalar_tensor_tensor(out=dtmp[:, 1, :], in0=d, scalar=1.0, in1=dtmp[:, 0, :],
                                               op0=ALU.add, op1=ALU.add).then_inc(s_ds, 1)
                nc.vector.tensor_scalar(dtmp[:, 0, :], dtmp[:, 0, :], -1.0, 1.0, ALU.mult, ALU.add)\
                    .then_inc(s_dg, 1)

            s_dg = sem("degree_step")

            def l0_dis(q):
                dve.wait_ge(s_dp, q + 1)
                dve.wait_ge(s_dg, 3 * q + 3)
                nc.vector.tensor_tensor(dis[:, bass.ds(q * G, G)], dtmp[:, 2, :], dtmp[:, 0, :], ALU.mult)\
                    .then_inc(s_dis, 1)

            def l0_sum(q):
                dve.wait_ge(s_ag, q + 1)
                dve.wait_ge(s_x1t, q)
                nc.vector.tensor_tensor(y0[:, :, :], graphs_of(2), per_graph(rdeg), ALU.mult).then_inc(s_d0, 1)
                dve.wait_ge(s_d0, 3 * q + 1)
                nc.vector.tensor_tensor(y0[:, :, :], graphs_of(1), y0[:, :, :], ALU.add).then_inc(s_d0, 1)
                dve.wait_ge(s_d0, 3 * q + 2)
                nc.vector.scalar_tensor_tensor(out=y0[:, :, :], in0=y0[:, :, :], scalar=0.0, in1=cols(x_all, q),
                                               op0=ALU.max, op1=ALU.add).then_inc(s_d0, 1)
                dve.wait_ge(s_d0, 3 * q + 3)
                norm_stats(0, y0, q)

            def l0_norm(q):
                normalise(0, y0, q, s_x1)
                wait_apart(s_x1, q + 1)
                nc.vector.tensor_copy(cols(x_all, q), y0[:, :, :]).then_inc(s_x1k, 1)

            def l1_scores(q):
                dve.wait_ge(s_h, q + 1)
                dve.wait_ge(s_src, q + 1)
                dve.wait_ge(s_at, q)
                nc.vector.tensor_reduce(soft[:, 0, :], graphs_of(4), AX.X, ALU.max).then_inc(s_sf, 1)
                nc.vector.tensor_tensor(att[:, :, :], graphs_of(4), per_graph(src), ALU.add).then_inc(s_sf, 1)
                dve.wait_ge(s_sf, 4 * q + 1)
                nc.vector.scalar_tensor_tensor(out=soft[:, 3, :], in0=src[:, :], scalar=-1.0, in1=soft[:, 0, :],
                                               op0=ALU.mult, op1=ALU.subtract).then_inc(s_sf, 1)
                dve.wait_ge(s_sf, 4 * q + 3)
                nc.vector.scalar_tensor_tensor(out=soft[:, 1, :], in0=soft[:, 3, :], scalar=SLOPE, in1=soft[:, 3, :],
                                               op0=ALU.mult, op1=ALU.min).then_inc(s_sf, 1)
                dve.wait_ge(s_sf, 4 * q + 4)
                nc.vector.scalar_tensor_tensor(out=att[:, :, :], in0=att[:, :, :], scalar=SLOPE, in1=att[:, :, :],
                                               op0=ALU.mult, op1=ALU.max).then_inc(s_nm, 1)

            s_sf = sem("softmax_step")
            s_rd = sem("denominator_inverted")

            def l1_attention(q):
                dve.wait_ge(s_ex, q + 1)
                nc.vector.reciprocal(soft[:, 4, :], soft[:, 2, :]).then_inc(s_rd, 1)
                dve.wait_ge(s_rd, q + 1)
                for g in range(G):
                    last = nc.vector.scalar_tensor_tensor(
                        out=att[:, g, :], in0=att[:, g, :], scalar=soft[:, 4, g:g + 1],
                        in1=adj_all[:, bass.ds(q * G + g, 1), :].rearrange("p g n -> p (g n)"),
                        op0=ALU.mult, op1=ALU.add)
                last.then_inc(s_att, 1)

            def l1_sum(q):
                dve.wait_ge(s_xr, q + 1)
                nc.vector.scalar_tensor_tensor(out=y1[:, :, :], in0=graphs_of(3), scalar=SLOPE, in1=y1[:, :, :],
                                               op0=ALU.mult, op1=ALU.add).then_inc(s_d1, 1)
                dve.wait_ge(s_d1, q + 1)
                norm_stats(1, y1, q)

            def l1_norm(q):
                normalise(1, y1, q, s_x2)
                wait_apart(s_x2, q + 1)
                nc.vector.tensor_copy(cols(x_all, q), y1[:, :, :]).then_inc(s_x2k, 1)

            def l2_sum(q):
                dve.wait_ge(s_cv, q + 1)
                dve.wait_ge(s_x3t, q)
                dve.wait_ge(s_x3b, q)
                nc.vector.tensor_tensor(y2[:, :, :], graphs_of(6), supp[:, :, :], ALU.add).then_inc(s_d2, 1)
                dve.wait_ge(s_d2, 2 * q + 1)
                dve.wait_ge(s_xb, q + 1)
                for g in range(G):
                    last = nc.vector.scalar_tensor_tensor(out=y2[:, g, :], in0=y2[:, g, :],
                                                          scalar=dis[:, bass.ds(q * G + g, 1)], in1=x2b[:, g, :],
                                                          op0=ALU.mult, op1=ALU.add)
                last.then_inc(s_d2, 1)
                dve.wait_ge(s_d2, 2 * q + 2)
                norm_stats(2, y2, q)

            def l2_norm(q):
                normalise(2, y2, q, s_x3)
                dve.wait_ge(s_x3, q + 1)
                for g in range(G):
                    last = nc.vector.scalar_tensor_tensor(
                        out=x_all[:, bass.ds(q * G + g, 1), :].rearrange("p g n -> p (g n)"), in0=betaB[:, :],
                        scalar=deg[:, bass.ds(q * G + g, 1)], in1=y2[:, g, :], op0=ALU.mult, op1=ALU.add)
                last.then_inc(s_x3b, 1)

            def layers(t, l0, l1, l2):
                if l0: l0_degree(t)
                if l1: l1_scores(t - 1)
                if l0: l0_dis(t)
                if l1: l1_attention(t - 1)
                if l2: l2_sum(t - 2)
                if l0: l0_sum(t)
                if l2: l2_norm(t - 2)
                if l1: l1_sum(t - 1)
                if l0: l0_norm(t)
                if l1: l1_norm(t - 1)

            layers(0, True, False, False)
            layers(1, True, True, False)
            layers(2, True, True, True)
            with dve.Fori(3, GROUPS) as t:
                layers(t, True, True, True)
            layers(GROUPS, False, True, True)
            layers(GROUPS + 1, False, False, True)

            def reduce(g, c):
                slot = c % 2
                dve.wait_ge(s_half, g + 1)
                nc.vector.tensor_reduce(ss[:, slot, 0:WIDE], sq[:, slot, :, 0:P // 2], AX.X, ALU.add).then_inc(s_red, 1)

            def finish(b, k):
                if k == 0:
                    dve.wait_ge(s_acc, (b + 1) * P)
                    nc.vector.tensor_tensor(fin[:, 0, :], acc[:, 0, :], acc[:, 1, :], ALU.add).then_inc(s_fin, 1)
                if k == 1:
                    dve.wait_ge(s_gam, 2 * b + 2)
                    nc.vector.bn_stats(fst[:, :], fin[:, 2, :]).then_inc(s_fin, 1)
                if k == 2:
                    wait_apart(s_fin, 3 * b + 2)
                    nc.vector.bn_aggr(fmv[:, :], fst[:, :]).then_inc(s_fin, 1)
                if k == 3:
                    dve.wait_ge(s_fsd, b + 1)
                    nc.vector.reciprocal(fsd[:, 1:2], fsd[:, 0:1]).then_inc(s_frd, 1)
                if k == 4:
                    dve.wait_ge(s_frd, b + 1)
                    nc.vector.tensor_scalar(x_all[:, bass.ds(b, 1), :].rearrange("p g n -> p (g n)"), fin[:, 2, :],
                                            fmv[:, 0:1], fsd[:, 1:2], ALU.subtract, ALU.mult).then_inc(s_res, 1)

            s_frd = sem("finish_inverted")
            FINISH = {0: 0, 3: 1, 4: 2, 6: 3, 7: 4}

            def invert(g, c):
                slot = c % 2
                dve.wait_ge(s_sd, g + 1)
                nc.vector.reciprocal(rs[:, slot, :], sd[:, slot, :]).then_inc(s_inv, 1)

            def weigh(g, b, c):
                slot = c % 2
                dve.wait_ge(s_inv, g + 1)
                nc.vector.tensor_tensor(wt[:, slot, :], rs[:, slot, :],
                                        adj_all[:, bass.ds(b, 1), c * J:(c + 1) * J].rearrange("p g j -> p (g j)"),
                                        ALU.mult).then_inc(s_wk, 1)

            def edge_graph(b, first, last):
                for c in range(CHUNKS):
                    g = b * CHUNKS + c
                    slot = c % 2
                    if c in FINISH and not first:
                        finish(b - 1, FINISH[c])
                    dve.wait_ge(s_wk, g + 1)
                    for m in range(J):
                        a = acc[:, m % 2, :]
                        if m == REDUCE_AT and not (last and c == CHUNKS - 1):
                            reduce(g + 1, c + 1)
                        if c == 0 and m == 0 and not first:
                            dve.wait_ge(s_fin, 3 * b - 2)
                        if c == 0 and m < 2:
                            nc.vector.tensor_scalar(a, z_of(c, m), wt[:, slot, m:m + 1], None, ALU.mult)\
                                .then_inc(s_acc, 1)
                        else:
                            dve.wait_ge(s_acc, b * P + c * J + m - 1)
                            nc.vector.scalar_tensor_tensor(out=a, in0=z_of(c, m), scalar=wt[:, slot, m:m + 1], in1=a,
                                                           op0=ALU.mult, op1=ALU.add).then_inc(s_acc, 1)
                        if m == INVERT_AT and not (last and c == CHUNKS - 1):
                            invert(g + 1, c + 1)
                        if m == WEIGH_AT and not (last and c == CHUNKS - 1):
                            weigh(g + 1, b + (c + 1) // CHUNKS, (c + 1) % CHUNKS)

            reduce(0, 0)
            invert(0, 0)
            weigh(0, 0, 0)
            edge_graph(0, True, False)
            with dve.Fori(1, GRAPHS - 1) as b:
                edge_graph(b, False, False)
            edge_graph(GRAPHS - 1, False, True)
            for k in range(5):
                finish(GRAPHS - 1, k)


_INS = ['x', 'adj', 'L0_gnn_W', 'L0_gnn_b', 'L1_gnn_W', 'L1_gnn_a', 'L2_gnn_weight', 'L2_gnn_bias', 'L3_gnn_W1',
        'L3_gnn_b1', 'L3_gnn_W2', 'L3_gnn_b2', 'L3_gnn_gamma', 'L3_gnn_beta']
_OUTS = [((64, 128, 128), 'float32')]


def kernel(**inputs):
    import numpy as _np
    import concourse.bacc as _bacc
    from concourse import mybir as _mybir
    from concourse.bass_utils import run_bass_kernel_spmd as _run

    nc = _bacc.Bacc("TRN2", target_bir_lowering=False, num_devices=1)
    arrays, args = {}, []
    for name in _INS:
        a = _np.ascontiguousarray(inputs[name])
        arrays[f"in_{name}_dram"] = a
        args.append(nc.dram_tensor(f"in_{name}_dram", a.shape, _mybir.dt.from_np(a.dtype), kind="ExternalInput").ap())
    for i, (shape, dtype) in enumerate(_OUTS):
        dt = _mybir.dt.from_np(_np.dtype(dtype))
        args.append(nc.dram_tensor(f"out_{i}_dram", shape, dt, kind="ExternalOutput").ap())
    graph_layers_kernel(nc, *args)
    r = _run(nc, [arrays], core_ids=[0])
    return r.results[0]["out_0_dram"]
```

```python
from contextlib import ExitStack

import concourse.bass as bass
from concourse import mybir

F32 = mybir.dt.float32
BF16 = mybir.dt.bfloat16
ALU = mybir.AluOpType
ACT = mybir.ActivationFunctionType
AX = mybir.AxisListType

EPS = 1e-5
SLOPE = 0.2


def graph_layers_kernel(nc, x, adj, w0, b0, w1, a1, w2, b2, e_w1, e_b1, e_w2, e_b2, e_gamma, e_beta, out):
    GRAPHS, N, D = x.shape
    P = 128
    assert N == P and D == P
    G = 4
    GROUPS = GRAPHS // G
    GW = G * P
    J = 16
    CHUNKS = P // J
    BANK = 4
    BANKS = J // BANK
    PIECE = 8
    PIECES = P // PIECE
    PER = J // PIECE
    WIDE = 8
    REDUCE_AT = 10
    INVERT_AT = 12
    WEIGH_AT = 14
    HR = 4
    AHEAD = 2

    with ExitStack() as ctx:
        def sb(name, shape, dt=F32):
            return ctx.enter_context(nc.sbuf_tensor(name, shape, dt))

        def sem(name):
            return ctx.enter_context(nc.semaphore(name))

        adj_all = sb("adj_all", [P, GRAPHS, P])
        x_all = sb("x_all", [P, GRAPHS, P])
        aT_all = sb("aT_all", [P, GRAPHS, P])
        bT_all = sb("bT_all", [P, GRAPHS, P])
        ident = sb("ident", [P, P])
        ones16 = sb("ones16", [P, P], BF16)
        w0_sb = sb("w0_sb", [P, 2 * P])
        w0T = sb("w0T", [P, 2, P])
        w1_sb = sb("w1_sb", [P, P])
        a1B = sb("a1B", [P, 2 * P])
        u = sb("u", [P, 2])
        uB = sb("uB", [P, 2, P])
        w2_sb = sb("w2_sb", [P, P])
        b2B = sb("b2B", [P, P])
        e_w1_sb = sb("e_w1_sb", [P, 2, P])
        e_b1_sb = sb("e_b1_sb", [P, 1])
        e_w2_sb = sb("e_w2_sb", [P, P])
        w2c = sb("w2c", [P, P])
        rowB = sb("rowB", [P, 2, P])
        rowH = sb("rowH", [P, 3, 2, P], BF16)
        bias16 = sb("bias16", [P, 2, BANK, P], BF16)
        gammaB = sb("gammaB", [P, P])
        betaB = sb("betaB", [P, P])
        mean_c = sb("mean_c", [P, 2])
        eps_c = sb("eps_c", [P, 1])
        half_c = sb("half_c", [P, G])
        hid = sb("hid", [P, HR, PIECE, P])
        xq = sb("xq", [P, G, P])
        adjq = sb("adjq", [P, G, P])
        xT = hid[:, 0, 0:G, :]
        proj = sb("proj", [P, G, P])
        y0 = sb("y0", [P, G, P])
        x1T = sb("x1T", [P, G, P])
        h1 = sb("h1", [P, G, P])
        att = sb("att", [P, G, P])
        attT = sb("attT", [P, G, P])
        y1 = sb("y1", [P, G, P])
        x2T = sb("x2T", [P, G, P])
        adjr = sb("adjr", [P, G, P])
        adjT = sb("adjT", [P, G, P])
        supp = sb("supp", [P, G, P])
        y2 = sb("y2", [P, G, P])
        x2b = sb("x2b", [P, G, P])
        x3T = sb("x3T", [P, G, P])
        deg = sb("deg", [P, GRAPHS])
        rdeg = sb("rdeg", [P, G])
        dis = sb("dis", [P, GRAPHS])
        dtmp = sb("dtmp", [P, 3, G])
        soft = sb("soft", [P, 4, G])
        lnst = [sb(f"lnst{k}", [P, G, 6]) for k in range(3)]
        lnmv = [sb(f"lnmv{k}", [P, G, 2]) for k in range(3)]
        lnve = [sb(f"lnve{k}", [P, G]) for k in range(3)]
        lnnm = [sb(f"lnnm{k}", [P, G]) for k in range(3)]
        lnrs = [sb(f"lnrs{k}", [P, 2, G]) for k in range(3)]
        sq = sb("sq", [P, 2, WIDE, P])
        junk = sb("junk", [P, J - WIDE, P])
        ss = sb("ss", [P, 2, J])
        sd = sb("sd", [P, 2, J])
        rs = sb("rs", [P, 2, J])
        wt = sb("wt", [P, 2, J])
        acc = sb("acc", [P, 4, P])
        fin = sb("fin", [P, 3, P])
        carrier = sb("carrier", [P, 2])
        fst = sb("fst", [P, 6])
        fmv = sb("fmv", [P, 2])
        fsd = sb("fsd", [P, 2])

        psum = ctx.enter_context(nc.psum_tensor("psum", [P, 8, 512], F32))
        bank = [psum[:, k, :] for k in range(8)]

        def z_of(c, m, n=1):
            at = (c % 2) * J + m
            return psum[:, :, :].rearrange("p k n -> p (k n)")[:, at * P:(at + n) * P]

        def graphs_of(k):
            return bank[k][:, :].rearrange("p (g n) -> p g n", g=G)

        def per_graph(t):
            return t[:, :].unsqueeze(2).to_broadcast([P, G, P])

        s_w = sem("weights_loaded")
        s_cst = sem("constants_set")
        s_wT = sem("w0_transposed")
        s_set = sem("setup_step")
        s_wready = sem("weights_ready")
        s_xq = sem("x_group_loaded")
        s_aq = sem("adj_group_loaded")
        s_r = sem("adj_again_loaded")
        s_all = sem("kept_inputs_loaded")
        s_xt = sem("xT_in_psum")
        s_xte = sem("xT_ready")
        s_xp = sem("self_and_neighbour_products")
        s_pe = sem("proj_ready")
        s_ag = sem("aggregated_in_psum")
        s_d0 = sem("vector_L0_step")
        s_rs = [sem(f"rsqrt_ready{k}") for k in range(3)]
        s_ve = [sem(f"variance_ready{k}") for k in range(3)]
        s_pw = [sem(f"power_ready{k}") for k in range(3)]
        s_ds = sem("degree_shifted")
        s_dp = sem("degree_power")
        s_dis = sem("dis_ready")
        s_x1 = sem("x1_ready")
        s_x1k = sem("x1_kept")
        s_x1t = sem("x1T_in_psum")
        s_x1e = sem("x1T_ready")
        s_h = sem("h_in_psum")
        s_e = sem("scores_in_psum")
        s_he = sem("h_ready")
        s_sc = sem("scores_copied")
        s_lk = sem("leaky_scores_ready")
        s_d1 = sem("vector_L1_step")
        s_ex = sem("exp_ready")
        s_att = sem("attention_ready")
        s_at = sem("attention_T_in_psum")
        s_ate = sem("attention_T_ready")
        s_mh = sem("attended_in_psum")
        s_rl = sem("attended_relu_ready")
        s_xr = sem("x1_plus_relu_ready")
        s_x2 = sem("x2_ready")
        s_x2k = sem("x2_kept")
        s_x2t = sem("x2T_in_psum")
        s_x2e = sem("x2T_ready")
        s_tr = sem("adjT_in_psum")
        s_tre = sem("adjT_ready")
        s_su = sem("support_in_psum")
        s_sue = sem("support_ready")
        s_xb = sem("x2_plus_bias_ready")
        s_cv = sem("convolved_in_psum")
        s_d2 = sem("vector_L2_step")
        s_x3 = sem("x3_ready")
        s_x3t = sem("x3T_in_psum")
        s_x3e = sem("x3T_ready")
        s_ab = sem("a_and_b_in_psum")
        s_abe = sem("a_and_b_ready")
        s_x3b = sem("residual_ready")
        s_pre = sem("sums_ready")
        s_hid = sem("hidden_ready")
        s_z = sem("z_bank_ready")
        s_sq = sem("squares_ready")
        s_half = sem("squares_halved")
        s_red = sem("squares_summed")
        s_ac = sem("accumulated_squares")
        s_sd = sem("deviation_ready")
        s_inv = sem("deviation_inverted")
        s_wk = sem("weights_of_chunk_ready")
        s_acc = sem("z_accumulated")
        s_fin = sem("finish_step")
        s_gam = sem("scaled_and_residual_added")
        s_fsd = sem("finish_deviation")
        s_res = sem("result_ready")
        s_out = sem("result_stored")

        def cols(t, q):
            return t[:, bass.ds(q * G, G), :]

        def free(engine, s, count):
            if not isinstance(count, int) or count > 0:
                engine.wait_ge(s, count)

        def upto(count):
            return min(count, GROUPS) if isinstance(count, int) else count

        LAGS = 5

        def run_layers(engine, steps):
            for t in range(LAGS + 1):
                steps(t, [0 <= t - lag < GROUPS for lag in range(LAGS + 1)])
            with engine.Fori(LAGS + 1, GROUPS) as t:
                steps(t, [True] * (LAGS + 1))
            for t in range(GROUPS, GROUPS + LAGS - 1):
                steps(t, [0 <= t - lag < GROUPS for lag in range(LAGS + 1)])

        LAST = GROUPS - 1

        block = ctx.enter_context(nc.Block())

        @block.sync
        def _(sp):
            def row(ap):
                return ap.rearrange("(a n) -> a n", a=1).to_broadcast([P, ap.shape[0]])

            for dst, s in ((w0_sb[:, :], w0), (w1_sb[:, :], w1), (w2_sb[:, :], w2),
                           (e_w1_sb[:, :, :], e_w1.rearrange("(t h) k -> h t k", t=2)),
                           (e_w2_sb[:, :], e_w2), (e_b1_sb[:, :], e_b1.rearrange("(k a) -> k a", a=1)),
                           (a1B[:, :], row(a1)), (b2B[:, :], row(b2)), (gammaB[:, :], row(e_gamma)),
                           (betaB[:, :], row(e_beta)), (rowB[:, 0, :], row(b0)), (rowB[:, 1, :], row(e_b2))):
                sp.dma_start(dst, s).then_inc(s_w, 16)

            def group(t, q):
                return t[bass.ds(q * G, G), :, :].rearrange("g n d -> n g d")

            def kept(q):
                sp.wait_ge(s_all, q * 32)
                sp.dma_start(cols(x_all, q), group(x, q)).then_inc(s_all, 16)
                sp.dma_start(cols(adj_all, q), group(adj, q)).then_inc(s_all, 16)

            def for_l0(q):
                sp.wait_ge(s_xq, q * 16)
                sp.wait_ge(s_xt, q)
                sp.dma_start(xq[:, :, :], group(x, q)).then_inc(s_xq, 16)
                sp.wait_ge(s_aq, q * 16)
                sp.wait_ge(s_ag, q)
                sp.dma_start(adjq[:, :, :], group(adj, q)).then_inc(s_aq, 16)

            def for_l2(q):
                sp.wait_ge(s_r, q * 16)
                sp.wait_ge(s_tr, q)
                sp.dma_start(adjr[:, :, :], group(adj, q)).then_inc(s_r, 16)

            for q in range(4):
                for_l0(q)
                kept(q)
            for_l2(0)
            with sp.Fori(4, GROUPS) as q:
                kept(q)
                for_l0(q)
                for_l2(q - 3)
            for q in range(GROUPS - 3, GROUPS):
                for_l2(q)
            with sp.Fori(0, GRAPHS) as b:
                sp.wait_ge(s_res, b + 1)
                sp.dma_start(out[bass.ds(b, 1), :, :].rearrange("g n d -> n g d"),
                             x_all[:, bass.ds(b, 1), :]).then_inc(s_out, 16)
            sp.wait_ge(s_out, 16 * GRAPHS)

        @block.tensor
        def _(pe):
            def transposes(k, source):
                for g in range(G):
                    last = nc.tensor.transpose(bank[k][:, g * P:(g + 1) * P], source[:, g, :], ident[:, :])
                return last

            pe.wait_ge(s_w, 16 * 12)
            pe.wait_ge(s_cst, 1)
            nc.tensor.transpose(bank[0][:, 0:P], w0_sb[:, 0:P], ident[:, :])
            nc.tensor.transpose(bank[0][:, P:2 * P], w0_sb[:, P:2 * P], ident[:, :]).then_inc(s_wT, 1)
            pe.wait_ge(s_wready, 1)

            def l0_transpose(q):
                pe.wait_ge(s_xq, (q + 1) * 16)
                free(pe, s_x1e, q - 1)
                transposes(0, xq).then_inc(s_xt, 1)

            def l0_project(q):
                pe.wait_ge(s_xte, q + 1)
                free(pe, s_d0, 3 * q - 1)
                nc.tensor.matmul(bank[1][:, :], ones16[:, :], bias16[:, 0, :, :], start=True, stop=False,
                                 skip_group_check=True)
                for g in range(G):
                    nc.tensor.matmul(bank[1][:, g * P:(g + 1) * P], xT[:, g, :], w0T[:, 0, :],
                                     start=False, stop=(g == G - 1), skip_group_check=True)
                for g in range(G):
                    last = nc.tensor.matmul(bank[2][:, g * P:(g + 1) * P], xT[:, g, :], w0T[:, 1, :],
                                            start=True, stop=True)
                last.then_inc(s_xp, 1)

            def l0_aggregate(q):
                pe.wait_ge(s_aq, (q + 1) * 16)
                pe.wait_ge(s_pe, q + 1)
                for g in range(G):
                    last = nc.tensor.matmul(bank[2][:, g * P:(g + 1) * P], adjq[:, g, :], proj[:, g, :],
                                            start=True, stop=True)
                last.then_inc(s_ag, 1)

            def l0_x1T(q):
                pe.wait_ge(s_x1, q + 1)
                pe.wait_ge(s_xte, upto(q + 2))
                transposes(0, y0).then_inc(s_x1t, 1)

            def l1_h(q):
                pe.wait_ge(s_x1e, q + 1)
                free(pe, s_x2e, q - 1)
                for g in range(G):
                    last = nc.tensor.matmul(bank[5][:, g * P:(g + 1) * P], x1T[:, g, :], w1_sb[:, :],
                                            start=True, stop=True)
                last.then_inc(s_h, 1)

            def l1_scores(q):
                pe.wait_ge(s_x1e, q + 1)
                pe.wait_ge(s_ate, q)
                nc.tensor.matmul(bank[4][:, :], uB[:, 1, :], x1T[:, :, :], start=True, stop=False,
                                 skip_group_check=True)
                for g in range(G):
                    last = nc.tensor.matmul(bank[4][:, g * P:(g + 1) * P], x1T[:, g, :], uB[:, 0, :],
                                            start=False, stop=(g == G - 1), skip_group_check=True)
                last.then_inc(s_e, 1)

            def l1_transpose(q):
                pe.wait_ge(s_att, q + 1)
                transposes(4, att).then_inc(s_at, 1)

            def l1_attend(q):
                pe.wait_ge(s_ate, q + 1)
                pe.wait_ge(s_he, q + 1)
                free(pe, s_d1, q)
                for g in range(G):
                    last = nc.tensor.matmul(bank[3][:, g * P:(g + 1) * P], attT[:, g, :], h1[:, g, :],
                                            start=True, stop=True)
                last.then_inc(s_mh, 1)

            def l1_x2T(q):
                pe.wait_ge(s_x2, q + 1)
                pe.wait_ge(s_he, upto(q + 2))
                transposes(5, y1).then_inc(s_x2t, 1)

            def l2_adjT(q):
                pe.wait_ge(s_r, (q + 1) * 16)
                free(pe, s_d2, q)
                transposes(6, adjr).then_inc(s_tr, 1)

            def l2_support(q):
                pe.wait_ge(s_x2e, q + 1)
                free(pe, s_abe, q - 1)
                for g in range(G):
                    last = nc.tensor.matmul(bank[7][:, g * P:(g + 1) * P], x2T[:, g, :], w2_sb[:, :],
                                            start=True, stop=True)
                last.then_inc(s_su, 1)

            def l2_convolve(q):
                pe.wait_ge(s_tre, q + 1)
                pe.wait_ge(s_sue, q + 1)
                free(pe, s_abe, q)
                nc.tensor.matmul(bank[6][:, :], ident[:, :], supp[:, :, :], start=True, stop=False,
                                 skip_group_check=True)
                for g in range(G):
                    last = nc.tensor.matmul(bank[6][:, g * P:(g + 1) * P], adjT[:, g, :], supp[:, g, :],
                                            start=False, stop=(g == G - 1), skip_group_check=True)
                last.then_inc(s_cv, 1)

            def l2_x3T(q):
                pe.wait_ge(s_x3, q + 1)
                pe.wait_ge(s_tre, upto(q + 2))
                transposes(6, y2).then_inc(s_x3t, 1)

            def l3_inputs(q):
                pe.wait_ge(s_x3e, q + 1)
                pe.wait_ge(s_sue, upto(q + 2))
                nc.tensor.matmul(bank[6][:, :], e_w1_sb[:, 0, :], x3T[:, :, :], start=True, stop=True)
                nc.tensor.matmul(bank[7][:, :], e_w1_sb[:, 1, :], x3T[:, :, :], start=True, stop=True)\
                    .then_inc(s_ab, 1)

            def layers(t, on):
                if on[3]: l1_transpose(t - 3)
                if on[4]: l2_support(t - 4)
                if on[3]: l1_attend(t - 3)
                if on[4]: l2_adjT(t - 4)
                if on[2]: l1_scores(t - 2)
                if on[5]: l2_x3T(t - 5)
                if on[2]: l1_h(t - 2)
                if on[0]: l0_transpose(t)
                if on[5]: l3_inputs(t - 5)
                if on[0]: l0_project(t)
                if on[4]: l2_convolve(t - 4)
                if on[0]: l0_aggregate(t)
                if on[3]: l1_x2T(t - 3)
                if on[1]: l0_x1T(t - 1)

            run_layers(pe, layers)

            def edge_chunks(b, chunks, first):
                for c in chunks:
                    for k in range(BANKS):
                        piece = c * PER + k * BANK // PIECE
                        if k * BANK % PIECE == 0:
                            pe.wait_ge(s_hid, b * PIECES + piece + 1)
                        if not (first and c < 2):
                            pe.wait_ge(s_acc, b * P + (c - 2) * J + (k + 1) * BANK)
                        nc.tensor.matmul(z_of(c, k * BANK, BANK), ones16[:, :], bias16[:, 1, :, :],
                                         start=True, stop=False, skip_group_check=True)
                        for m in range(BANK):
                            last = nc.tensor.matmul(z_of(c, k * BANK + m),
                                                    hid[:, piece % HR, (k * BANK + m) % PIECE, :], w2c[:, :],
                                                    start=False, stop=(m == BANK - 1), skip_group_check=True)
                        last.then_inc(s_z, 1)

            pe.wait_ge(s_x1e, GROUPS)
            pe.wait_ge(s_d0, 3 * GROUPS)
            pe.wait_ge(s_d1, GROUPS)
            edge_chunks(0, range(1), True)
            l2_x3T(LAST)
            l3_inputs(LAST)
            pe.wait_ge(s_abe, GROUPS)
            edge_chunks(0, range(1, CHUNKS), True)
            with pe.Fori(1, GRAPHS) as b:
                edge_chunks(b, range(CHUNKS), False)

        @block.scalar
        def _(act):
            def copy_bank(dst, k):
                return nc.scalar.activation(dst, graphs_of(k), ACT.Copy)

            act.wait_ge(s_wT, 1)
            nc.scalar.activation(w0T[:, :, :], bank[0][:, 0:2 * P].rearrange("p (t n) -> p t n", t=2), ACT.Copy)\
                .then_inc(s_set, 1)

            def normalise(k, y, q, done):
                act.wait_ge(s_rs[k], q + 1)
                for g in range(G):
                    last = nc.scalar.activation(y[:, g, :], y[:, g, :], ACT.Identity, bias=lnrs[k][:, 1, g:g + 1],
                                                scale=lnrs[k][:, 0, g:g + 1])
                last.then_inc(done, 1)

            def keep(y, q, ready, done):
                act.wait_ge(ready, q + 1)
                nc.scalar.activation(cols(x_all, q), y[:, :, :], ACT.Copy).then_inc(done, 1)

            def l0_xT(q):
                act.wait_ge(s_xt, q + 1)
                act.wait_ge(s_xp, q)
                copy_bank(xT[:, :, :], 0).then_inc(s_xte, 1)

            def l0_proj(q):
                act.wait_ge(s_xp, q + 1)
                act.wait_ge(s_ag, q)
                copy_bank(proj[:, :, :], 2).then_inc(s_pe, 1)

            def l0_x1T(q):
                act.wait_ge(s_x1t, q + 1)
                act.wait_ge(s_e, q)
                act.wait_ge(s_h, q)
                copy_bank(x1T[:, :, :], 0).then_inc(s_x1e, 1)

            def l1_h(q):
                act.wait_ge(s_h, q + 1)
                act.wait_ge(s_mh, q)
                copy_bank(h1[:, :, :], 5).then_inc(s_he, 1)

            def l1_scores(q):
                act.wait_ge(s_e, q + 1)
                act.wait_ge(s_at, q)
                copy_bank(att[:, :, :], 4).then_inc(s_sc, 1)

            def l1_exp(q):
                act.wait_ge(s_lk, q + 1)
                for g in range(G):
                    last = nc.scalar.activation(att[:, g, :], att[:, g, :], ACT.Exp, bias=soft[:, 1, g:g + 1],
                                                accum_out=soft[:, 2, g:g + 1])
                last.then_inc(s_ex, 1)

            def l1_attT(q):
                act.wait_ge(s_at, q + 1)
                act.wait_ge(s_mh, q)
                copy_bank(attT[:, :, :], 4).then_inc(s_ate, 1)

            def l1_relu(q):
                act.wait_ge(s_mh, q + 1)
                act.wait_ge(s_x2t, q)
                act.wait_ge(s_x2k, q)
                nc.scalar.activation(y1[:, :, :], graphs_of(3), ACT.Relu, scale=1.0 - SLOPE).then_inc(s_rl, 1)

            def l1_x2T(q):
                act.wait_ge(s_x2t, q + 1)
                act.wait_ge(s_su, q)
                copy_bank(x2T[:, :, :], 5).then_inc(s_x2e, 1)

            def l2_adjT(q):
                act.wait_ge(s_tr, q + 1)
                act.wait_ge(s_cv, q)
                copy_bank(adjT[:, :, :], 6).then_inc(s_tre, 1)

            def l2_support(q):
                act.wait_ge(s_su, q + 1)
                act.wait_ge(s_dis, q + 1)
                act.wait_ge(s_cv, q)
                for g in range(G):
                    last = nc.scalar.activation(supp[:, g, :], bank[7][:, g * P:(g + 1) * P], ACT.Copy,
                                                scale=dis[:, bass.ds(q * G + g, 1)])
                last.then_inc(s_sue, 1)

            def l2_x3T(q):
                act.wait_ge(s_x3t, q + 1)
                act.wait_ge(s_ab, q)
                copy_bank(x3T[:, :, :], 6).then_inc(s_x3e, 1)

            def l3_inputs(q):
                act.wait_ge(s_ab, q + 1)
                nc.scalar.activation(cols(aT_all, q), graphs_of(6), ACT.Identity, bias=e_b1_sb[:, 0:1])
                copy_bank(cols(bT_all, q), 7).then_inc(s_abe, 1)

            def layers(t, on):
                if on[3]: l1_attT(t - 3)
                if on[4]: l2_support(t - 4)
                if on[3]: l1_relu(t - 3)
                if on[4]: l2_adjT(t - 4)
                if on[5]: normalise(2, y2, t - 5, s_x3)
                if on[2]: l1_scores(t - 2)
                if on[5]: l2_x3T(t - 5)
                if on[0]: l0_xT(t)
                if on[1]: normalise(0, y0, t - 1, s_x1)
                if on[5]: l3_inputs(t - 5)
                if on[2]: l1_exp(t - 2)
                if on[2]: l1_h(t - 2)
                if on[0]: l0_proj(t)
                if on[3]: normalise(1, y1, t - 3, s_x2)
                if on[3]: keep(y1, t - 3, s_x2, s_x2k)
                if on[1]: keep(y0, t - 1, s_x1, s_x1k)
                if on[3]: l1_x2T(t - 3)
                if on[1]: l0_x1T(t - 1)

            run_layers(act, layers)

            def relu(n, h):
                act.wait_ge(s_pre, n + 1)
                nc.scalar.activation(hid[:, h % HR, :, :], hid[:, h % HR, :, :], ACT.Relu).then_inc(s_hid, 1)

            SPLIT = 8

            def squares(g, c, part):
                slot = c % 2
                if part == 0:
                    act.wait_ge(s_z, BANKS * g + (WIDE + BANK - 1) // BANK)
                    nc.scalar.activation(sq[:, slot, :, :], z_of(c, 0, WIDE).rearrange("p (m l) -> p m l", m=WIDE),
                                         ACT.Square).then_inc(s_sq, 1)
                for m in (range(WIDE, SPLIT), range(SPLIT, J))[part]:
                    if m % BANK == 0:
                        act.wait_ge(s_z, BANKS * g + m // BANK + 1)
                    last = nc.scalar.activation(junk[:, m - WIDE, :], z_of(c, m), ACT.Square,
                                                accum_out=ss[:, slot, m:m + 1])
                if part == 1:
                    last.then_inc(s_ac, 1)

            def deviation(g, c):
                slot = c % 2
                act.wait_ge(s_red, g + 1)
                act.wait_ge(s_ac, g + 1)
                nc.scalar.activation(sd[:, slot, :], ss[:, slot, :], ACT.Sqrt, bias=eps_c[:, 0:1], scale=1.0 / P)\
                    .then_inc(s_sd, 1)

            def finish_deviation(b):
                act.wait_ge(s_fin, 3 * b + 3)
                nc.scalar.activation(fsd[:, 0:1], fmv[:, 1:2], ACT.Sqrt, bias=eps_c[:, 0:1]).then_inc(s_fsd, 1)

            def edge_chunks(b, chunks, first, last):
                for c in chunks:
                    g = b * CHUNKS + c
                    for part in range(PER):
                        squares(g, c, part)
                        h = c * PER + part + AHEAD
                        if not (last and h >= PIECES):
                            relu(b * PIECES + h, h)
                    deviation(g, c)
                    if c == 5 and not first:
                        finish_deviation(b - 1)

            for c in range(AHEAD):
                relu(c, c)
            normalise(2, y2, LAST, s_x3)
            squares(0, 0, 0)
            relu(2, 2)
            l2_x3T(LAST)
            squares(0, 0, 1)
            relu(3, 3)
            l3_inputs(LAST)
            deviation(0, 0)
            edge_chunks(0, range(1, CHUNKS), True, False)
            with act.Fori(1, GRAPHS - 1) as b:
                edge_chunks(b, range(CHUNKS), False, False)
            edge_chunks(GRAPHS - 1, range(CHUNKS), False, True)
            finish_deviation(GRAPHS - 1)

        @block.gpsimd
        def _(pool):
            nc.gpsimd.memset(ident[:, :], 0.0).then_inc(s_set, 1)
            nc.gpsimd.memset(half_c[:, :], -0.5).then_inc(s_set, 1)
            nc.gpsimd.memset(eps_c[:, :], EPS).then_inc(s_set, 1)
            nc.gpsimd.memset(ones16[:, :], 1.0).then_inc(s_set, 1)
            nc.gpsimd.memset(bias16[:, :, :, :], 0.0).then_inc(s_set, 1)
            pool.wait_ge(s_set, 5)
            nc.gpsimd.affine_select(out=ident[:, :], in_=ident[:, :], compare_op=ALU.not_equal, fill=1.0,
                                    base=0, pattern=[[-1, P]], channel_multiplier=1).then_inc(s_cst, 1)

            def rsqrt(k, q):
                pool.wait_ge(s_ve[k], q + 1)
                nc.gpsimd.tensor_tensor(lnrs[k][:, 0, :], lnve[k][:, :], half_c[:, :], ALU.pow).then_inc(s_pw[k], 1)
                pool.wait_ge(s_pw[k], q + 1)
                nc.gpsimd.tensor_tensor(lnrs[k][:, 1, :], lnrs[k][:, 0, :], lnnm[k][:, :], ALU.mult)\
                    .then_inc(s_rs[k], 1)

            def degree(q):
                pool.wait_ge(s_ds, q + 1)
                nc.gpsimd.tensor_tensor(dtmp[:, 2, :], dtmp[:, 1, :], half_c[:, :], ALU.pow).then_inc(s_dp, 1)

            def l1_residual(q):
                pool.wait_ge(s_rl, q + 1)
                pool.wait_ge(s_x1k, q + 1)
                nc.gpsimd.tensor_tensor(y1[:, :, :], y1[:, :, :], cols(x_all, q), ALU.add).then_inc(s_xr, 1)

            def l2_bias(q):
                pool.wait_ge(s_x2k, q + 1)
                pool.wait_ge(s_d2, q)
                nc.gpsimd.tensor_tensor(x2b[:, :, :], cols(x_all, q),
                                        b2B[:, :].unsqueeze(1).to_broadcast([P, G, P]), ALU.add).then_inc(s_xb, 1)

            pool.wait_ge(s_wready, 1)

            def layers(t, on):
                if on[5]: rsqrt(2, t - 5)
                if on[3]: l1_residual(t - 3)
                if on[1]: rsqrt(0, t - 1)
                if on[4]: l2_bias(t - 4)
                if on[3]: rsqrt(1, t - 3)
                if on[0]: degree(t)

            run_layers(pool, layers)

            def sums(b, h, first):
                if not (first and h < HR):
                    pool.wait_ge(s_z, (b * PIECES + h - HR + 1) * (PIECE // BANK))
                nc.gpsimd.tensor_tensor(hid[:, h % HR, :, :],
                                        aT_all[:, bass.ds(b, 1), :].to_broadcast([P, PIECE, P]),
                                        bT_all[:, bass.ds(b, 1), h * PIECE:(h + 1) * PIECE]
                                        .rearrange("p g j -> p (g j)").unsqueeze(2).to_broadcast([P, PIECE, P]),
                                        ALU.add).then_inc(s_pre, 1)

            def scale(b):
                pool.wait_ge(s_fin, 3 * b + 1)
                nc.gpsimd.tensor_tensor(fin[:, 1, :], fin[:, 0, :], gammaB[:, :], ALU.mult).then_inc(s_gam, 1)
                pool.wait_ge(s_gam, 2 * b + 1)
                nc.gpsimd.tensor_tensor(fin[:, 2, :], fin[:, 1, :],
                                        x_all[:, bass.ds(b, 1), :].rearrange("p g n -> p (g n)"), ALU.add)\
                    .then_inc(s_gam, 1)

            def halve(g, c):
                slot = c % 2
                pool.wait_ge(s_sq, g + 1)
                nc.gpsimd.tensor_tensor(sq[:, slot, :, 0:P // 2], sq[:, slot, :, 0:P // 2], sq[:, slot, :, P // 2:P],
                                        ALU.add).then_inc(s_half, 1)

            SCALE_AT = 6
            pool.wait_ge(s_abe, 1)
            pool.wait_ge(s_xp, GROUPS)
            for h in range(HR):
                sums(0, h, True)
            rsqrt(2, LAST)
            halve(0, 0)
            pool.wait_ge(s_abe, GROUPS)
            for h in range(HR, PIECES):
                sums(0, h, True)
                if h > HR and h % PER == 0:
                    halve((h - HR) // PER, (h - HR) // PER)
            with pool.Fori(1, GRAPHS) as b:
                for h in range(PIECES):
                    sums(b, h, False)
                    if h % PER == 0:
                        halve(b * CHUNKS + (h - HR) // PER, (h - HR) // PER)
                    if h == SCALE_AT:
                        scale(b - 1)
            for c in range(CHUNKS - HR // PER, CHUNKS):
                halve((GRAPHS - 1) * CHUNKS + c, c)
            scale(GRAPHS - 1)

        @block.vector
        def _(dve):
            steps = [0]
            s_v = sem("vector_setup")

            def step(ins):
                steps[0] += 1
                ins.then_inc(s_v, 1)
                dve.wait_ge(s_v, steps[0])

            dve.wait_ge(s_w, 16 * 12)
            dve.wait_ge(s_cst, 1)
            step(nc.vector.memset(carrier[:, :], 0.0))
            for t in range(2):
                step(nc.vector.tensor_tensor_reduce(junk[:, 0, :], w1_sb[:, :], a1B[:, t * P:(t + 1) * P], 1.0, 0.0,
                                                    ALU.mult, ALU.add, u[:, t:t + 1]))
            step(nc.vector.tensor_copy(uB[:, :, :], u[:, :].unsqueeze(2).to_broadcast([P, 2, P])))
            step(nc.vector.tensor_reduce(mean_c[:, 0:1], e_w2_sb[:, :], AX.X, ALU.add))
            step(nc.vector.tensor_reduce(mean_c[:, 1:2], rowB[:, 1, :], AX.X, ALU.add))
            step(nc.vector.tensor_scalar(mean_c[:, :], mean_c[:, :], 1.0 / P, None, ALU.mult))
            step(nc.vector.tensor_scalar(w2c[:, :], e_w2_sb[:, :], mean_c[:, 0:1], None, ALU.subtract))
            step(nc.vector.tensor_scalar(rowB[:, 1, :], rowB[:, 1, :], mean_c[:, 1:2], None, ALU.subtract))
            rest = rowB
            for k in range(3):
                step(nc.vector.tensor_copy(rowH[:, k, :, :], rest[:, :, :]))
                step(nc.vector.tensor_tensor(fin[:, 0:2, :], rest[:, :, :], rowH[:, k, :, :], ALU.subtract))
                rest = fin[:, 0:2, :]
                row = slice(32 * k, 32 * k + 1)
                for t in range(2):
                    step(nc.vector.tensor_copy(bias16[row, t, :, :],
                                               rowH[row, k, t, :].unsqueeze(1).to_broadcast([1, BANK, P])))
            dve.wait_ge(s_set, 6)
            nc.vector.tensor_copy(carrier[:, 1:2], carrier[:, 0:1]).then_inc(s_wready, 1)

            def norm_stats(k, y, q):
                for g in range(G):
                    last = nc.vector.bn_stats(lnst[k][:, g, :], y[:, g, :])
                last.then_inc(s_ln[k], 1)
                wait_apart(s_ln[k], 2 * q + 1)
                for g in range(G):
                    last = nc.vector.bn_aggr(lnmv[k][:, g, :], lnst[k][:, g, :])
                last.then_inc(s_ln[k], 1)
                dve.wait_ge(s_ln[k], 2 * q + 2)
                nc.vector.tensor_scalar(lnnm[k][:, :], lnmv[k][:, :, 0], -1.0, None, ALU.mult)
                nc.vector.tensor_scalar(lnve[k][:, :], lnmv[k][:, :, 1], EPS, None, ALU.add).then_inc(s_ve[k], 1)

            def wait_apart(s, count):
                dve.wait_ge(s, count)
                nc.vector.tensor_copy(carrier[:, 1:2], carrier[:, 0:1])

            s_ln = [sem(f"norm_step{k}") for k in range(3)]

            def l0_degree(q):
                dve.wait_ge(s_all, (q + 1) * 32)
                d = deg[:, bass.ds(q * G, G)]
                nc.vector.tensor_reduce(d, cols(adj_all, q), AX.X, ALU.add).then_inc(s_dg, 1)
                dve.wait_ge(s_dg, 3 * q + 1)
                nc.vector.tensor_scalar(dtmp[:, 0, :], d, 1.0, 0.0, ALU.add, ALU.is_equal).then_inc(s_dg, 1)
                nc.vector.reciprocal(rdeg[:, :], d)
                dve.wait_ge(s_dg, 3 * q + 2)
                nc.vector.scalar_tensor_tensor(out=dtmp[:, 1, :], in0=d, scalar=1.0, in1=dtmp[:, 0, :],
                                               op0=ALU.add, op1=ALU.add).then_inc(s_ds, 1)
                nc.vector.tensor_scalar(dtmp[:, 0, :], dtmp[:, 0, :], -1.0, 1.0, ALU.mult, ALU.add)\
                    .then_inc(s_dg, 1)

            s_dg = sem("degree_step")

            def l0_dis(q):
                dve.wait_ge(s_dp, q + 1)
                dve.wait_ge(s_dg, 3 * q + 3)
                nc.vector.tensor_tensor(dis[:, bass.ds(q * G, G)], dtmp[:, 2, :], dtmp[:, 0, :], ALU.mult)\
                    .then_inc(s_dis, 1)

            def l0_sum(q):
                dve.wait_ge(s_ag, q + 1)
                dve.wait_ge(s_x1t, q)
                dve.wait_ge(s_x1k, q)
                nc.vector.tensor_tensor(y0[:, :, :], graphs_of(2), per_graph(rdeg), ALU.mult).then_inc(s_d0, 1)
                dve.wait_ge(s_d0, 3 * q + 1)
                nc.vector.tensor_tensor(y0[:, :, :], graphs_of(1), y0[:, :, :], ALU.add).then_inc(s_d0, 1)
                dve.wait_ge(s_d0, 3 * q + 2)
                nc.vector.scalar_tensor_tensor(out=y0[:, :, :], in0=y0[:, :, :], scalar=0.0, in1=cols(x_all, q),
                                               op0=ALU.max, op1=ALU.add).then_inc(s_d0, 1)
                dve.wait_ge(s_d0, 3 * q + 3)
                norm_stats(0, y0, q)

            def l1_scores(q):
                dve.wait_ge(s_sc, q + 1)
                nc.vector.tensor_reduce(soft[:, 0, :], graphs_of(4), AX.X, ALU.max, negate=True).then_inc(s_sf, 1)
                nc.vector.scalar_tensor_tensor(out=att[:, :, :], in0=graphs_of(4), scalar=SLOPE, in1=att[:, :, :],
                                               op0=ALU.mult, op1=ALU.max)
                dve.wait_ge(s_sf, q + 1)
                nc.vector.scalar_tensor_tensor(out=soft[:, 1, :], in0=soft[:, 0, :], scalar=SLOPE, in1=soft[:, 0, :],
                                               op0=ALU.mult, op1=ALU.min).then_inc(s_lk, 1)

            s_sf = sem("softmax_step")
            s_rd = sem("denominator_inverted")

            def l1_attention(q):
                dve.wait_ge(s_ex, q + 1)
                nc.vector.reciprocal(soft[:, 3, :], soft[:, 2, :]).then_inc(s_rd, 1)
                dve.wait_ge(s_rd, q + 1)
                for g in range(G):
                    last = nc.vector.scalar_tensor_tensor(
                        out=att[:, g, :], in0=att[:, g, :], scalar=soft[:, 3, g:g + 1],
                        in1=adj_all[:, bass.ds(q * G + g, 1), :].rearrange("p g n -> p (g n)"),
                        op0=ALU.mult, op1=ALU.add)
                last.then_inc(s_att, 1)

            def l1_sum(q):
                dve.wait_ge(s_xr, q + 1)
                nc.vector.scalar_tensor_tensor(out=y1[:, :, :], in0=graphs_of(3), scalar=SLOPE, in1=y1[:, :, :],
                                               op0=ALU.mult, op1=ALU.add).then_inc(s_d1, 1)
                dve.wait_ge(s_d1, q + 1)
                norm_stats(1, y1, q)

            def l2_sum(q):
                dve.wait_ge(s_cv, q + 1)
                dve.wait_ge(s_x3t, q)
                dve.wait_ge(s_x3b, q)
                dve.wait_ge(s_xb, q + 1)
                for g in range(G):
                    last = nc.vector.scalar_tensor_tensor(out=y2[:, g, :], in0=bank[6][:, g * P:(g + 1) * P],
                                                          scalar=dis[:, bass.ds(q * G + g, 1)], in1=x2b[:, g, :],
                                                          op0=ALU.mult, op1=ALU.add)
                last.then_inc(s_d2, 1)
                dve.wait_ge(s_d2, q + 1)
                norm_stats(2, y2, q)

            def l2_keep(q):
                dve.wait_ge(s_x3, q + 1)
                for g in range(G):
                    last = nc.vector.scalar_tensor_tensor(
                        out=x_all[:, bass.ds(q * G + g, 1), :].rearrange("p g n -> p (g n)"), in0=betaB[:, :],
                        scalar=deg[:, bass.ds(q * G + g, 1)], in1=y2[:, g, :], op0=ALU.mult, op1=ALU.add)
                last.then_inc(s_x3b, 1)

            def layers(t, on):
                if on[5]: l2_sum(t - 5)
                if on[1]: l0_dis(t - 1)
                if on[1]: l0_sum(t - 1)
                if on[3]: l1_sum(t - 3)
                if on[2]: l1_scores(t - 2)
                if on[5]: l2_keep(t - 5)
                if on[0]: l0_degree(t)
                if on[2]: l1_attention(t - 2)

            run_layers(dve, layers)

            def reduce(g, c):
                slot = c % 2
                dve.wait_ge(s_half, g + 1)
                nc.vector.tensor_reduce(ss[:, slot, 0:WIDE], sq[:, slot, :, 0:P // 2], AX.X, ALU.add).then_inc(s_red, 1)

            def finish(b, k):
                if k == 0:
                    dve.wait_ge(s_acc, (b + 1) * P)
                    nc.vector.tensor_tensor(fin[:, 0, :], acc[:, 0, :], acc[:, 1, :], ALU.add).then_inc(s_fin, 1)
                if k == 1:
                    dve.wait_ge(s_gam, 2 * b + 2)
                    nc.vector.bn_stats(fst[:, :], fin[:, 2, :]).then_inc(s_fin, 1)
                if k == 2:
                    nc.vector.bn_aggr(fmv[:, :], fst[:, :]).then_inc(s_fin, 1)
                if k == 3:
                    dve.wait_ge(s_fsd, b + 1)
                    nc.vector.reciprocal(fsd[:, 1:2], fsd[:, 0:1]).then_inc(s_frd, 1)
                if k == 4:
                    dve.wait_ge(s_frd, b + 1)
                    nc.vector.tensor_scalar(x_all[:, bass.ds(b, 1), :].rearrange("p g n -> p (g n)"), fin[:, 2, :],
                                            fmv[:, 0:1], fsd[:, 1:2], ALU.subtract, ALU.mult).then_inc(s_res, 1)

            s_frd = sem("finish_inverted")
            FINISH = {0: 0, 3: 1, 4: 2, 6: 3, 7: 4}

            FINISH_AFTER = 3

            def invert(g, c):
                slot = c % 2
                dve.wait_ge(s_sd, g + 1)
                nc.vector.reciprocal(rs[:, slot, :], sd[:, slot, :]).then_inc(s_inv, 1)

            def weigh(g, b, c):
                slot = c % 2
                dve.wait_ge(s_inv, g + 1)
                nc.vector.tensor_tensor(wt[:, slot, :], rs[:, slot, :],
                                        adj_all[:, bass.ds(b, 1), c * J:(c + 1) * J].rearrange("p g j -> p (g j)"),
                                        ALU.mult).then_inc(s_wk, 1)

            def edge_graph(b, first, last):
                for c in range(CHUNKS):
                    g = b * CHUNKS + c
                    slot = c % 2
                    dve.wait_ge(s_wk, g + 1)
                    for m in range(J):
                        if m == REDUCE_AT and not (last and c == CHUNKS - 1):
                            reduce(g + 1, c + 1)
                        if c == 0 and m < 2:
                            nc.vector.tensor_scalar(acc[:, 2 + m, :], z_of(c, m), wt[:, slot, m:m + 1], None, ALU.mult)\
                                .then_inc(s_acc, 1)
                        else:
                            if c == 0 and m == 2 and not first:
                                dve.wait_ge(s_fin, 3 * b - 2)
                            if c in FINISH and FINISH[c] == 2 and m == FINISH_AFTER and not first:
                                dve.wait_ge(s_fin, 3 * b - 1)
                            dve.wait_ge(s_acc, b * P + c * J + m - 1)
                            a = acc[:, m % 2, :]
                            before = acc[:, m, :] if c == 0 and m < 4 else a
                            nc.vector.scalar_tensor_tensor(out=a, in0=z_of(c, m), scalar=wt[:, slot, m:m + 1],
                                                           in1=before, op0=ALU.mult, op1=ALU.add).then_inc(s_acc, 1)
                        if c in FINISH and m == (0 if FINISH[c] == 0 else FINISH_AFTER) and not first:
                            finish(b - 1, FINISH[c])
                        if m == INVERT_AT and not (last and c == CHUNKS - 1):
                            invert(g + 1, c + 1)
                        if m == WEIGH_AT and not (last and c == CHUNKS - 1):
                            weigh(g + 1, b + (c + 1) // CHUNKS, (c + 1) % CHUNKS)

            l2_sum(LAST)
            reduce(0, 0)
            l2_keep(LAST)
            invert(0, 0)
            weigh(0, 0, 0)
            edge_graph(0, True, False)
            with dve.Fori(1, GRAPHS - 1) as b:
                edge_graph(b, False, False)
            edge_graph(GRAPHS - 1, False, True)
            for k in range(5):
                if k == 2:
                    dve.wait_ge(s_fin, 3 * GRAPHS - 1)
                finish(GRAPHS - 1, k)


_INS = ['x', 'adj', 'L0_gnn_W', 'L0_gnn_b', 'L1_gnn_W', 'L1_gnn_a', 'L2_gnn_weight', 'L2_gnn_bias', 'L3_gnn_W1',
        'L3_gnn_b1', 'L3_gnn_W2', 'L3_gnn_b2', 'L3_gnn_gamma', 'L3_gnn_beta']
_OUTS = [((64, 128, 128), 'float32')]


def kernel(**inputs):
    import numpy as _np
    import concourse.bacc as _bacc
    from concourse import mybir as _mybir
    from concourse.bass_utils import run_bass_kernel_spmd as _run

    nc = _bacc.Bacc("TRN2", target_bir_lowering=False, num_devices=1)
    arrays, args = {}, []
    for name in _INS:
        a = _np.ascontiguousarray(inputs[name])
        arrays[f"in_{name}_dram"] = a
        args.append(nc.dram_tensor(f"in_{name}_dram", a.shape, _mybir.dt.from_np(a.dtype), kind="ExternalInput").ap())
    for i, (shape, dtype) in enumerate(_OUTS):
        dt = _mybir.dt.from_np(_np.dtype(dtype))
        args.append(nc.dram_tensor(f"out_{i}_dram", shape, dt, kind="ExternalOutput").ap())
    graph_layers_kernel(nc, *args)
    r = _run(nc, [arrays], core_ids=[0])
    return r.results[0]["out_0_dram"]
```
